# Optimizing a Trainium2 kernel written in Bass

```python
import numpy as np
import jax
import jax.numpy as jnp

def _softmax(x, axis=-1):
    return jax.nn.softmax(x, axis=axis)

def _gelu(x):
    return jax.nn.gelu(x, approximate=True)

def _silu(x):
    return jax.nn.silu(x)

def _sigmoid(x):
    return jax.nn.sigmoid(x)

def _layernorm(x, axis=-1, eps=1e-05):
    m = jnp.mean(x, axis=axis, keepdims=True)
    v = jnp.var(x, axis=axis, keepdims=True)
    return (x - m) / jnp.sqrt(v + eps)

def _scatter_add(tgt, idx, src, axis=0):
    return tgt.at[idx].add(src)

def _segment_sum(src, seg, n):
    return jax.ops.segment_sum(src, seg, n)
kernel_name = 'mk_sandwich_d1_jaxref_r4_cadaa4'

def setup_inputs(seed: int=0):
    np.random.seed(seed)
    _w = jnp.asarray

    def _L0_attn_setup():
        import math
        import jax, jax.numpy as jnp
        import numpy as np
        D_MODEL = 512
        NUM_HEADS = 16
        D_HEAD = D_MODEL // NUM_HEADS
        THETA = 10000.0

        def _rope_tables(seq_len, d_head):
            idx = jnp.arange(0, d_head, 2, dtype=jnp.float32)
            inv_freq = THETA ** (-idx / d_head)
            angles = jnp.arange(seq_len, dtype=jnp.float32)[:, None] * inv_freq[None, :]
            return (jnp.cos(angles), jnp.sin(angles))

        def _apply_rope(x, cos, sin):
            B, H, S, d = x.shape
            xp = x.reshape(B, H, S, d // 2, 2)
            xe, xo = (xp[..., 0], xp[..., 1])
            rot = jnp.stack([xe * cos - xo * sin, xe * sin + xo * cos], axis=-1)
            return rot.reshape(B, H, S, d)
        key = jax.random.key(seed)
        k_x, k_q, k_k, k_v, k_o = jax.random.split(key, 5)
        std = math.sqrt(2.0 / (D_MODEL + D_MODEL))
        x = jax.random.normal(k_x, (4, 512, D_MODEL), dtype=jnp.float32)
        Wq = jax.random.normal(k_q, (D_MODEL, D_MODEL), dtype=jnp.float32) * std
        Wk = jax.random.normal(k_k, (D_MODEL, D_MODEL), dtype=jnp.float32) * std
        Wv = jax.random.normal(k_v, (D_MODEL, D_MODEL), dtype=jnp.float32) * std
        Wo = jax.random.normal(k_o, (D_MODEL, D_MODEL), dtype=jnp.float32) * std
        return {'x': x, 'Wq': Wq, 'Wk': Wk, 'Wv': Wv, 'Wo': Wo}
    _L0_attn_in = _L0_attn_setup()

    def _L0_ffn_setup():
        import jax, jax.numpy as jnp
        import numpy as np
        E = 64
        K = 8
        D = 512
        F = 128
        FS = 128
        key = jax.random.key(seed)
        ks = jax.random.split(key, 9)
        s = 0.02
        return {'x': jax.random.normal(ks[0], (2, 256, D), jnp.float32), 'router_w': jax.random.normal(ks[1], (E, D), jnp.float32) * s, 'Wg': jax.random.normal(ks[2], (E, F, D), jnp.float32) * s, 'Wu': jax.random.normal(ks[3], (E, F, D), jnp.float32) * s, 'Wd': jax.random.normal(ks[4], (E, D, F), jnp.float32) * s, 'Wsg': jax.random.normal(ks[5], (FS, D), jnp.float32) * s, 'Wsu': jax.random.normal(ks[6], (FS, D), jnp.float32) * s, 'Wsd': jax.random.normal(ks[7], (D, FS), jnp.float32) * s, 'Wse': jax.random.normal(ks[8], (1, D), jnp.float32) * s}
    _L0_ffn_in = _L0_ffn_setup()
    _d = {'L0_attn_x': _L0_attn_in['x'], 'L0_attn_Wq': _L0_attn_in['Wq'], 'L0_attn_Wk': _L0_attn_in['Wk'], 'L0_attn_Wv': _L0_attn_in['Wv'], 'L0_attn_Wo': _L0_attn_in['Wo'], 'L0_ffn_router_w': _L0_ffn_in['router_w'], 'L0_ffn_Wg': _L0_ffn_in['Wg'], 'L0_ffn_Wu': _L0_ffn_in['Wu'], 'L0_ffn_Wd': _L0_ffn_in['Wd'], 'L0_ffn_Wsg': _L0_ffn_in['Wsg'], 'L0_ffn_Wsu': _L0_ffn_in['Wsu'], 'L0_ffn_Wsd': _L0_ffn_in['Wsd'], 'L0_ffn_Wse': _L0_ffn_in['Wse']}
    _x0 = _d['L0_attn_x']
    _d['L0_attn_x'] = jax.random.normal(jax.random.fold_in(jax.random.key(seed), 1), (4, 512, 512), dtype=_x0.dtype)
    del _x0
    return _d

def reference(L0_attn_x, L0_attn_Wq, L0_attn_Wk, L0_attn_Wv, L0_attn_Wo, L0_ffn_router_w, L0_ffn_Wg, L0_ffn_Wu, L0_ffn_Wd, L0_ffn_Wsg, L0_ffn_Wsu, L0_ffn_Wsd, L0_ffn_Wse):

    def _L0_attn_ref(x, Wq, Wk, Wv, Wo):
        import math
        import jax, jax.numpy as jnp
        import numpy as np
        D_MODEL = 512
        NUM_HEADS = 16
        D_HEAD = D_MODEL // NUM_HEADS
        THETA = 10000.0

        def _rope_tables(seq_len, d_head):
            idx = jnp.arange(0, d_head, 2, dtype=jnp.float32)
            inv_freq = THETA ** (-idx / d_head)
            angles = jnp.arange(seq_len, dtype=jnp.float32)[:, None] * inv_freq[None, :]
            return (jnp.cos(angles), jnp.sin(angles))

        def _apply_rope(x, cos, sin):
            B, H, S, d = x.shape
            xp = x.reshape(B, H, S, d // 2, 2)
            xe, xo = (xp[..., 0], xp[..., 1])
            rot = jnp.stack([xe * cos - xo * sin, xe * sin + xo * cos], axis=-1)
            return rot.reshape(B, H, S, d)
        B, S, D = x.shape
        H, dh = (NUM_HEADS, D_HEAD)

        def proj(W):
            y = jnp.einsum('bsi,oi->bso', x, W)
            return y.reshape(B, S, H, dh).transpose(0, 2, 1, 3)
        q, k, v = (proj(Wq), proj(Wk), proj(Wv))
        cos, sin = _rope_tables(S, dh)
        q = _apply_rope(q, cos, sin)
        k = _apply_rope(k, cos, sin)
        scores = jnp.einsum('bhqd,bhkd->bhqk', q.astype(jnp.float32), k.astype(jnp.float32)) / math.sqrt(dh)
        causal = jnp.tril(jnp.ones((S, S), dtype=bool))
        scores = jnp.where(causal, scores, jnp.finfo(jnp.float32).min)
        probs = jax.nn.softmax(scores, axis=-1).astype(v.dtype)
        attn = jnp.einsum('bhqk,bhkd->bhqd', probs, v)
        attn = attn.transpose(0, 2, 1, 3).reshape(B, S, D)
        return jnp.einsum('bsi,oi->bso', attn, Wo)

    def _L0_ffn_ref(x, router_w, Wg, Wu, Wd, Wsg, Wsu, Wsd, Wse):
        import jax, jax.numpy as jnp
        import numpy as np
        E = 64
        K = 8
        D = 512
        F = 128
        FS = 128
        B, S, _ = x.shape
        T = B * S
        xt = x.reshape(T, D)
        logits = xt @ router_w.T
        probs = jax.nn.softmax(logits.astype(jnp.float32), axis=-1)
        top_w, top_i = jax.lax.top_k(probs, K)
        top_w = top_w / jnp.sum(top_w, axis=-1, keepdims=True)
        comb = jnp.zeros((T, E), jnp.float32)
        comb = comb.at[jnp.arange(T)[:, None], top_i].set(top_w)
        comb = comb.astype(x.dtype)

        def step(acc, ws):
            wg_e, wu_e, wd_e, we = ws
            h = jax.nn.silu(xt @ wg_e.T) * (xt @ wu_e.T) @ wd_e.T
            return (acc + we[:, None] * h, None)
        routed, _ = jax.lax.scan(step, jnp.zeros_like(xt), (Wg, Wu, Wd, comb.T))
        shared = jax.nn.silu(xt @ Wsg.T) * (xt @ Wsu.T) @ Wsd.T
        shared = jax.nn.sigmoid(xt @ Wse.T) * shared
        return (routed + shared).reshape(B, S, D)
    x = L0_attn_x
    x = x + _layernorm(_L0_attn_ref(_layernorm(x, axis=-1), L0_attn_Wq, L0_attn_Wk, L0_attn_Wv, L0_attn_Wo), axis=-1)
    x = x + _layernorm(_L0_ffn_ref(_layernorm(x, axis=-1), L0_ffn_router_w, L0_ffn_Wg, L0_ffn_Wu, L0_ffn_Wd, L0_ffn_Wsg, L0_ffn_Wsu, L0_ffn_Wsd, L0_ffn_Wse), axis=-1)
    return x

_drawn_inputs = setup_inputs


def setup_inputs(seed=0):
    import zlib

    import numpy as np

    out = dict(_drawn_inputs(seed))
    spreads = {}
    factors = {}
    for name, (base, spread) in spreads.items():
        noise = np.random.default_rng([zlib.crc32(name.encode()), seed]).standard_normal(out[name].shape)
        drawn = base * np.exp(spread * noise) if base else spread * noise
        out[name] = jnp.asarray(drawn.astype(out[name].dtype))
    for name, factor in factors.items():
        out[name] = (out[name] * factor).astype(out[name].dtype)
    return out
```

```python
from contextlib import ExitStack

import numpy as np

import concourse.bass as bass
from concourse import mybir

FP32 = mybir.dt.float32
ACT = mybir.ActivationFunctionType
ALU = mybir.AluOpType
AX = mybir.AxisListType

P = 128
B, S, D = 4, 512, 512
H, DH = 16, 32
E, K, F = 64, 8, 128
THETA = 10000.0
EPS = 1e-5
TB = S // P
TILES = B * TB
DC = D // P
HG = P // DH
G = H // HG
QKV = 3 * P
UNITS = H * TB
GU = UNITS // G
GATEUP = 2 * F
MASKED = -1.0e38
SCALE = float(DH) ** -0.5


def misc_steps(g, s, last):
    if g < G - 1:
        return [(k, t) for t in range(TB) for k, at in (("proj", 3 * t), ("qkt", 3 * t + 2)) if at == s]
    if last:
        return []
    return [(k, t) for t in range(TB) for k, at in (("xt", 4 * t), ("proj", 4 * t + 1), ("qkt", 4 * t + 3)) if at == s]


def sandwich_kernel(nc, x, wqkv, wo, router, experts, rope, mask, headmask, ident, out):
    ctx = ExitStack()
    with ctx:
        def sb(name, shape):
            return ctx.enter_context(nc.sbuf_tensor(name, shape, FP32))

        def sem(name):
            return ctx.enter_context(nc.semaphore(name))

        x_sb = sb("x_sb", [P, TILES, D])
        attn_t = sb("attn_t", [P, G, B * S])
        x2_t = sb("x2_t", [P, DC, B * S])
        wqkv_sb = sb("wqkv_sb", [P, DC, G, QKV])
        wo_sb = sb("wo_sb", [P, G, D])
        router_sb = sb("router_sb", [P, DC, E + 1])
        rope_sb = sb("rope_sb", [P, TB, 2 * DH])
        mask_sb = sb("mask_sb", [P, S])
        hmask_sb = sb("hmask_sb", [P, HG])
        ident_sb = sb("ident_sb", [P, P])
        stats = sb("stats", [P, TILES, 6])
        moments = sb("moments", [P, TILES, 2])
        rstd = sb("rstd", [P, TILES])
        logits = sb("logits", [P, TILES, E + 1])
        comb = sb("comb", [P, TILES, E + 1])
        xn = sb("xn", [P, 2, D])
        x_t = sb("x_t", [P, DC, S])
        qkv = sb("qkv", [P, 2, TB, QKV])
        roped = sb("roped", [P, 2, 2 * P])
        rope_cos = sb("rope_cos", [P, 2 * P])
        rope_sin = sb("rope_sin", [P, 2 * P])
        k_t = sb("k_t", [P, 2, S])
        q_pad = sb("q_pad", [P, 2, HG, S])
        probs = sb("probs", [P, 4, S])
        neg_max = sb("neg_max", [P, 4])
        den = sb("den", [P, 4])
        rden = sb("rden", [P, 4])
        probs_t = x2_t[:, :, :].rearrange("p c n -> p (c n)")[:, 0:2 * TB * S].rearrange("p (a k n) -> p a k n", a=2, k=TB)
        acc = attn_t[:, :, :].rearrange("p g n -> p (g n)").rearrange("p (t n) -> p t n", n=D)
        w_exp = [wqkv_sb[:, :, :, :].rearrange("p c g n -> p (c g n)")[:, i * 1536:(i + 1) * 1536] for i in range(2)]
        gate = probs[:, 0:2, :]
        hidden = probs[:, 2:4, :]
        a_s = q_pad[:, :, :, :]
        x2 = xn
        x2t_s = qkv[:, :, :, :].rearrange("p a t n -> p (a t n)")[:, 0:2 * D].rearrange("p (a c n) -> p a c n", a=2, c=DC)
        delta = k_t[:, :, :]
        small = sb("small", [P, 2, 16])
        prob_e = qkv[:, :, :, :].rearrange("p a t n -> p (a t n)")[:, 2 * D:4 * D].rearrange("p (t e) -> p t e", e=E)
        prob_r = qkv[:, :, :, :].rearrange("p a t n -> p (a t n)")[:, 4 * D:6 * D].rearrange("p (t e) -> p t e", e=E)
        top = sb("top", [P, TILES, K])
        rt = sb("rt", [P, 6, TILES])

        ps = ctx.enter_context(nc.psum_tensor("ps", [P, 8, 512], FP32))
        s_bank = [ps[:, i, :] for i in range(4)]
        pt_bank = [ps[:, 4 + i, :] for i in range(2)]
        av_bank = ps[:, 6, :]
        misc = ps[:, 7, :]

        NIN = 8
        s_in = [sem(f"s_in{i}") for i in range(NIN)]
        s_xin = [sem(f"s_xin{i}") for i in range(B)]
        s_moments = sem("s_moments")
        s_ln = sem("s_ln")
        s_std = sem("s_std")
        s_xn = sem("s_xn")
        s_xt_ps = sem("s_xt_ps")
        s_xt = sem("s_xt")
        s_qkv_ps = sem("s_qkv_ps")
        s_qkv = sem("s_qkv")
        s_rtmp = sem("s_rtmp")
        s_rope = sem("s_rope")
        s_qkt_ps = sem("s_qkt_ps")
        s_qkt = sem("s_qkt")
        s_scored = sem("s_scored")
        s_masked = sem("s_masked")
        s_exp = sem("s_exp")
        s_recip = sem("s_recip")
        s_probs = sem("s_probs")
        s_turned = sem("s_turned")
        s_pt = sem("s_pt")
        s_av = sem("s_av")
        s_attn = sem("s_attn")
        s_stage = sem("s_stage")
        s_o = sem("s_o")
        s_d1 = sem("s_d1")
        s_var = sem("s_var")
        s_sq = sem("s_sq")
        s_x2 = sem("s_x2")
        s_x2t_ps = sem("s_x2t_ps")
        s_x2t = sem("s_x2t")
        s_x2all = sem("s_x2all")
        s_log_ps = sem("s_log_ps")
        s_log = sem("s_log")
        s_rd = sem("s_rd")
        s_re = sem("s_re")
        s_comb = sem("s_comb")
        s_comb2 = sem("s_comb2")
        s_fin2 = sem("s_fin2")
        s_w = [sem("s_w0"), sem("s_w1")]
        s_gu = sem("s_gu")
        s_silu = sem("s_silu")
        s_hid = sem("s_hid")
        s_down = sem("s_down")
        s_acc = sem("s_acc")
        s_fd = sem("s_fd")
        s_fs = sem("s_fs")
        s_fin = sem("s_fin")
        s_out = sem("s_out")

        block = ctx.enter_context(nc.Block())
        x_v = x.rearrange("(t p) d -> p t d", p=P)
        out_v = out.rearrange("(t p) d -> p t d", p=P)

        LOADS = [(ident_sb[:, :], ident), (rope_sb[:, :, :], rope), (hmask_sb[:, :], headmask),
                 (mask_sb[:, :], mask), (wo_sb[:, :, :], wo), (router_sb[:, :, :], router)]
        I_IDENT, I_ROPE, I_HMASK, I_MASK, I_WO, I_ROUTER, I_WQKV = range(7)

        EX = E + 1

        def every_batch(eng, body):
            with eng.Fori(0, B - 1) as b:
                body(b, False)
            body(B - 1, True)

        @block.sync
        def _(sp):
            sp.dma_start(x_sb[:, 0:TB, :], x_v[:, 0:TB, :]).then_inc(s_xin[0], 16)
            sp.dma_start(ident_sb[:, :], ident).then_inc(s_in[I_IDENT], 16)
            sp.dma_start(wqkv_sb[:, :, :, :], wqkv).then_inc(s_in[I_WQKV], 16)
            for i in range(1, 6):
                sp.dma_start(*LOADS[i]).then_inc(s_in[i], 16)
            for b in range(1, B):
                sp.dma_start(x_sb[:, b * TB:(b + 1) * TB, :], x_v[:, b * TB:(b + 1) * TB, :]).then_inc(s_xin[b], 16)
            sp.wait_ge(s_acc, 1)
            for p in range(2):
                sp.dma_start(w_exp[p], experts[p]).then_inc(s_w[p], 16)
            with sp.Fori(0, EX // 2 - 1) as j:
                for p in range(2):
                    sp.wait_ge(s_down, (j * 2 + (p + 1)) * TILES)
                    sp.dma_start(w_exp[p], experts[j * 2 + (p + 2)]).then_inc(s_w[p], 16)
            sp.wait_ge(s_down, (EX - 2) * TILES)
            sp.dma_start(w_exp[0], experts[EX - 1]).then_inc(s_w[0], 16)
            for i in range(TILES):
                sp.wait_ge(s_fin, i + 1)
                sp.dma_start(out_v[:, i, :], x_sb[:, i, :]).then_inc(s_out, 16)
            sp.wait_ge(s_out, 16 * TILES)

        @block.gpsimd
        def _(pool):
            def rope_group_tile(i4, g, t):
                n = (i4 + g) * TB + t
                src = qkv[:, g % 2, t, 0:2 * P]
                pair = src.rearrange("p (h j e) -> p h j e", h=2 * HG, e=2)
                sin_pair = rope_sin[:, :].rearrange("p (h j e) -> p h j e", h=2 * HG, e=2)
                heads = src.rearrange("p (h d) -> p h d", h=2 * HG)
                cos = rope_sb[:, t, 0:DH].rearrange("p (o d) -> p o d", o=1).broadcast_to([P, 2 * HG, DH])
                nsin = rope_sb[:, t, DH:DH + 16].rearrange("p (o d) -> p o d", o=1).broadcast_to([P, 2 * HG, 16])
                psin = rope_sb[:, t, DH + 16:DH + 32].rearrange("p (o d) -> p o d", o=1).broadcast_to([P, 2 * HG, 16])
                pool.wait_ge(s_qkv, n + 1)
                pool.tensor_tensor(out=rope_cos[:, :].rearrange("p (h d) -> p h d", h=2 * HG), in0=heads,
                                   in1=cos, op=ALU.mult).then_inc(s_rtmp, 1)
                pool.tensor_tensor(out=sin_pair[:, :, :, 0], in0=pair[:, :, :, 1], in1=nsin,
                                   op=ALU.mult).then_inc(s_rtmp, 1)
                pool.tensor_tensor(out=sin_pair[:, :, :, 1], in0=pair[:, :, :, 0], in1=psin,
                                   op=ALU.mult).then_inc(s_rtmp, 1)
                pool.wait_ge(s_rtmp, (n + 1) * 3)
                pool.tensor_tensor(out=roped[:, t % 2, :], in0=rope_cos[:, :], in1=rope_sin[:, :],
                                   op=ALU.add).then_inc(s_rope, 1)
                pool.wait_ge(s_rope, n + 1)

            pool.wait_ge(s_in[I_ROPE], 16)
            for t in range(TB):
                rope_group_tile(0, 0, t)

            def batch(b, last):
                for g in range(1, G + (not last)):
                    for t in range(TB):
                        rope_group_tile(b * G, g, t)

            every_batch(pool, batch)

            pool.wait_ge(s_attn, B * G)
            for j in range(TILES // 2):
                for p in range(2):
                    i = j * 2 + p
                    pool.tensor_copy(a_s[:, p, :, 0:P], attn_t[:, :, bass.ts(i, P)]).then_inc(s_stage, 1)
                    pool.wait_ge(s_o, i + 1)
                    pool.wait_ge(s_x2t, i + 1)
                    pool.tensor_copy(x2_t[:, :, bass.ts(i, P)], x2t_s[:, p, :, :]).then_inc(s_x2all, 1)

        @block.scalar
        def _(act):
            act.wait_ge(s_ln, 1)
            act.activation(rstd[:, :], moments[:, :, 1], ACT.Sqrt).then_inc(s_std, 1)

            def evac_xt(b4, t):
                act.wait_ge(s_xt_ps, b4 + t + 1)
                act.activation(x_t[:, :, bass.ts(t, P)], misc.rearrange("p (c n) -> p c n", c=DC),
                               ACT.Copy).then_inc(s_xt, 1)

            def evac_qkv(i4, g, t):
                n = (i4 + g) * TB + t
                act.wait_ge(s_qkv_ps, n + 1)
                act.activation(qkv[:, g % 2, t, :], misc[:, 0:QKV], ACT.Copy).then_inc(s_qkv, 1)

            for t in range(TB):
                evac_xt(0, t)
                evac_qkv(0, 0, t)

            def exp(b, u):
                act.wait_ge(s_masked, b * UNITS + (u + 1))
                n = (u % TB + 1) * P
                act.activation(probs[:, u % 4, 0:n], s_bank[u % 4][:, 0:n], ACT.Exp, bias=neg_max[:, u % 4:u % 4 + 1],
                               scale=-1.0, accum_out=den[:, u % 4:u % 4 + 1]).then_inc(s_exp, 1)

            def evac_pt(b, u):
                h, qt = divmod(u, TB)
                act.wait_ge(s_turned, b * UNITS + (u + 1))
                if h >= 2 and qt == 0:
                    act.wait_ge(s_av, b * H + (h - 1))
                act.activation(probs_t[:, h % 2, 0:qt + 1, bass.ts(qt, P)],
                               pt_bank[u % 2].rearrange("p (k n) -> p k n", k=TB)[:, 0:qt + 1, :],
                               ACT.Copy).then_inc(s_pt, 1)

            def evac_attn(b, g):
                act.wait_ge(s_av, b * H + HG * (g + 1))
                act.activation(attn_t[:, g, bass.ts(b, S)], av_bank, ACT.Copy).then_inc(s_attn, 1)

            def batch(b, last):
                exp(b, 0)
                exp(b, 1)
                for u in range(UNITS):
                    g, s = divmod(u, GU)
                    if u >= 1:
                        evac_pt(b, u - 1)
                    if u + 2 < UNITS:
                        exp(b, u + 2)
                    if s == 1 and g >= 1:
                        evac_attn(b, g - 1)
                    for kind, t in misc_steps(g, s, last):
                        if kind == "xt":
                            evac_xt((b + 1) * TB, t)
                        if kind == "proj":
                            evac_qkv(b * G, g + 1, t)
                evac_pt(b, UNITS - 1)
                evac_attn(b, G - 1)

            every_batch(act, batch)

            act.preload_act_table(ACT.Sqrt)
            for j in range(TILES // 2):
                for p in range(2):
                    i = j * 2 + p
                    for k in range(2):
                        act.wait_ge(s_var, i * 2 + (k + 1))
                        act.activation(small[:, p, 4 * k + 2:4 * k + 3], small[:, p, 4 * k + 1:4 * k + 2],
                                       ACT.Sqrt).then_inc(s_sq, 1)
                    act.wait_ge(s_x2t_ps, i + 1)
                    act.activation(x2t_s[:, p, :, :], ps[:, 2 + p, :].rearrange("p (c n) -> p c n", c=DC),
                                   ACT.Copy).then_inc(s_x2t, 1)
            act.wait_ge(s_rd, 1)
            for i in range(TILES):
                act.activation(prob_e[:, i, :], logits[:, i, 0:E], ACT.Exp, bias=rt[:, 0, i:i + 1],
                               accum_out=rt[:, 1, i:i + 1]).then_inc(s_re, 1)
            act.activation(rt[:, 4, :], logits[:, :, E], ACT.Exp, scale=-1.0).then_inc(s_re, 1)

            act.preload_act_table(ACT.Silu)

            def expert_act(e, p):
                for n in range(B):
                    act.wait_ge(s_gu, e * B + (n + 1))
                    act.activation(gate[:, n % 2, :], ps[:, n % 2, :], ACT.Silu).then_inc(s_silu, 1)

            with act.Fori(0, EX // 2) as j:
                for p in range(2):
                    expert_act(j * 2 + p, p)
            expert_act(EX - 1, 0)
            act.wait_ge(s_fd, 1)
            act.activation(rstd[:, :], moments[:, :, 1], ACT.Sqrt).then_inc(s_fs, 1)

        @block.tensor
        def _(pe):
            def xt(b4, t, first=False):
                pe.wait_ge(s_xn, b4 + t + 1)
                if not (first and t == 0):
                    pe.wait_ge(s_qkt, b4 * G + t)
                for c in range(DC):
                    mm = pe.transpose(misc[:, bass.ts(c, P)], xn[:, t % 2, bass.ts(c, P)], ident_sb[:, :])
                mm.then_inc(s_xt_ps, 1)

            def proj(i4, g, t, after_xt=None):
                if after_xt is not None:
                    pe.wait_ge(s_xt, after_xt + t + 1)
                else:
                    pe.wait_ge(s_qkt, (i4 + g) * TB + t)
                for c in range(DC):
                    mm = pe.matmul(misc[:, 0:QKV], x_t[:, c, bass.ts(t, P)], wqkv_sb[:, c, g % G, :],
                                   start=(c == 0), stop=(c == DC - 1))
                mm.then_inc(s_qkv_ps, 1)

            def qkt(i4, g, t):
                pe.wait_ge(s_rope, (i4 + g) * TB + (t + 1))
                for c in range(2):
                    mm = pe.transpose(misc[:, bass.ts(c, P)], roped[:, t % 2, bass.ts(c, P)], ident_sb[:, :])
                mm.then_inc(s_qkt_ps, 1)

            pe.wait_ge(s_in[I_IDENT], 16)
            for t in range(TB):
                xt(0, t, first=True)
                if t == 0:
                    pe.wait_ge(s_in[I_WQKV], 16)
                proj(0, 0, t, after_xt=0)
                qkt(0, 0, t)

            def score(b, u):
                g, (h, qt) = u // GU, divmod(u % GU, TB)
                pe.wait_ge(s_qkt, (b * G + g) * TB + (qt + 1))
                n = (qt + 1) * P
                pe.matmul(s_bank[u % 4][:, 0:n], q_pad[:, g % 2, h, bass.ts(qt, P)], k_t[:, g % 2, 0:n],
                          start=True, stop=True).then_inc(s_scored, 1)

            def turn(b, u):
                qt = u % TB
                pe.wait_ge(s_probs, b * UNITS + (u + 1))
                if u >= 2:
                    pe.wait_ge(s_pt, b * UNITS + (u - 1))
                for k in range(qt + 1):
                    mm = pe.transpose(pt_bank[u % 2][:, bass.ts(k, P)], probs[:, u % 4, bass.ts(k, P)], ident_sb[:, :])
                mm.then_inc(s_turned, 1)

            def weigh(b, h):
                g, hh = divmod(h, HG)
                pe.wait_ge(s_pt, b * UNITS + TB * (h + 1))
                if hh == 0 and g >= 1:
                    pe.wait_ge(s_attn, b * G + g)
                o = av_bank[DH * hh:DH * (hh + 1), :]
                for k in range(TB):
                    v0 = 2 * P + DH * hh
                    mm = pe.matmul(o[:, k * P:S], qkv[:, g % 2, k, v0:v0 + DH], probs_t[:, h % 2, k, k * P:S],
                                   start=(k == 0), stop=(k == TB - 1))
                mm.then_inc(s_av, 1)

            def batch(b, last):
                pe.wait_ge(s_qkt, (b * G) * TB + TB)
                for u in range(3):
                    score(b, u)
                for u in range(UNITS):
                    g, s = divmod(u, GU)
                    if u + 3 < UNITS:
                        score(b, u + 3)
                    turn(b, u)
                    if u >= TB and u % TB == 0:
                        weigh(b, u // TB - 1)
                    for kind, t in misc_steps(g, s, last):
                        if kind == "xt":
                            xt((b + 1) * TB, t)
                        if kind == "proj":
                            proj(b * G, g + 1, t, after_xt=(b + 1) * TB if g == G - 1 else None)
                        if kind == "qkt":
                            qkt(b * G, g + 1, t)
                weigh(b, H - 1)
                pe.wait_ge(s_attn, b * G + G)

            every_batch(pe, batch)

            pe.wait_ge(s_in[I_WO], 16)
            pe.wait_ge(s_in[I_ROUTER], 16)
            for j in range(TILES // 2):
                for p in range(2):
                    i = j * 2 + p
                    pe.wait_ge(s_stage, i + 1)
                    for g in range(G):
                        mm = pe.matmul(ps[:, p, :], a_s[:, p, g, 0:P], wo_sb[:, g, :], start=(g == 0), stop=(g == G - 1))
                    mm.then_inc(s_o, 1)
                    pe.wait_ge(s_x2, i + 1)
                    for c in range(DC):
                        mm = pe.transpose(ps[:, 2 + p, bass.ts(c, P)], x2[:, p, bass.ts(c, P)], ident_sb[:, :])
                    mm.then_inc(s_x2t_ps, 1)
                    pe.wait_ge(s_x2t, i + 1)
                    for c in range(DC):
                        mm = pe.matmul(ps[:, 4 + p, 0:E + 1], x2t_s[:, p, c, :], router_sb[:, c, :],
                                       start=(c == 0), stop=(c == DC - 1))
                    mm.then_inc(s_log_ps, 1)

            def gate_up(w, e, n):
                if n >= 2:
                    pe.wait_ge(s_hid, e * B + (n - 1))
                for half in range(2):
                    for c in range(DC):
                        mm = pe.matmul(ps[:, 2 * half + n % 2, :], w[:, c * GATEUP + half * F:c * GATEUP + (half + 1) * F],
                                       x2_t[:, c, bass.ts(n, S)], start=(c == 0), stop=(c == DC - 1))
                mm.then_inc(s_gu, 1)

            def down(w, e, n):
                pe.wait_ge(s_hid, e * B + (n + 1))
                for t in range(TB):
                    k = n * TB + t
                    if k == 0:
                        pe.wait_ge(s_acc, e * TILES + 1)
                    if k >= 4:
                        pe.wait_ge(s_acc, e * TILES + (k - 2))
                    pe.matmul(ps[:, 4 + k % 4, :], hidden[:, n % 2, bass.ts(t, P)], w[:, DC * GATEUP:DC * GATEUP + D],
                              start=True, stop=True).then_inc(s_down, 1)

            def expert_pe(j, p):
                e = j * 2 + p
                pe.wait_ge(s_w[p], (j + 1) * 16)
                gate_up(w_exp[p], e, 0)
                for n in range(B):
                    if n + 1 < B:
                        gate_up(w_exp[p], e, n + 1)
                    down(w_exp[p], e, n)

            pe.wait_ge(s_x2all, TILES)
            pe.wait_ge(s_log, TILES)
            with pe.Fori(0, EX // 2) as j:
                for p in range(2):
                    expert_pe(j, p)
            expert_pe(EX // 2, 0)

        @block.vector
        def _(dve):
            for b in range(B):
                dve.wait_ge(s_xin[b], 16)
                for t in range(b * TB, (b + 1) * TB):
                    dve.bn_stats(stats[:, t, :], x_sb[:, t, :]).then_inc(s_moments, 1)
            dve.wait_ge(s_moments, TILES)
            for t in range(TILES):
                dve.bn_aggr(moments[:, t, :], stats[:, t, :]).then_inc(s_moments, 1)
            dve.wait_ge(s_moments, 2 * TILES)
            dve.tensor_scalar(moments[:, :, 1], moments[:, :, 1], EPS, None, ALU.add).then_inc(s_ln, 1)
            dve.wait_ge(s_std, 1)
            dve.reciprocal(rstd[:, :], rstd[:, :]).then_inc(s_ln, 1)
            dve.wait_ge(s_ln, 2)

            def norm_x(b4, t, first=False):
                if not (first and t < 2):
                    dve.wait_ge(s_xt_ps, b4 + t - 1)
                m = b4 + t
                dve.tensor_scalar(xn[:, t % 2, :], _row(x_sb, m),
                                  _col2(moments, m, 0), _col(rstd, m), ALU.subtract, ALU.mult).then_inc(s_xn, 1)

            def _row(t, m):
                return t[:, m, :]

            def _col(t, m):
                return t[:, bass.ts(m, 1)]

            def _col2(t, m, k):
                return t[:, m, k:k + 1]

            def take_qkt(i4, g, t):
                n = (i4 + g) * TB + t
                dve.wait_ge(s_qkt_ps, n + 1)
                dve.tensor_copy(k_t[:, g % 2, bass.ts(t, P)], misc[:, P:2 * P])
                q = misc[:, 0:P].rearrange("p (o n) -> p o n", o=1).broadcast_to([P, HG, P])
                hm = hmask_sb[:, :].rearrange("p (h o) -> p h o", o=1).broadcast_to([P, HG, P])
                dve.tensor_tensor(out=q_pad[:, g % 2, :, bass.ts(t, P)], in0=q, in1=hm, op=ALU.mult).then_inc(s_qkt, 1)

            dve.wait_ge(s_in[I_HMASK], 16)
            for t in range(TB):
                norm_x(0, t, first=True)
                if t >= 1:
                    take_qkt(0, 0, t - 1)
            take_qkt(0, 0, TB - 1)
            dve.wait_ge(s_in[I_MASK], 16)

            def masked(u):
                n = (u % TB + 1) * P
                sc = s_bank[u % 4][:, 0:n]
                dve.tensor_tensor_reduce(sc, sc, mask_sb[:, S - n:S], -SCALE, 3.0e38, ALU.add, ALU.min,
                                         neg_max[:, u % 4:u % 4 + 1]).then_inc(s_masked, 1)

            def batch(b, last):
                dve.wait_ge(s_scored, b * UNITS + 2)
                dve.memset(rden[:, :], 0.0).then_inc(s_recip, 1)
                masked(0)
                masked(1)
                for u in range(UNITS):
                    g, s = divmod(u, GU)
                    k, n = u % 4, (u % TB + 1) * P
                    dve.wait_ge(s_exp, b * UNITS + (u + 1))
                    if u == 0:
                        dve.wait_ge(s_recip, b * (UNITS + 1) + 1)
                    dve.reciprocal(rden[:, k:k + 1], den[:, k:k + 1]).then_inc(s_recip, 1)
                    if u + 2 < UNITS:
                        dve.wait_ge(s_scored, b * UNITS + (u + 3))
                    dve.wait_ge(s_recip, b * (UNITS + 1) + (u + 2))
                    dve.tensor_scalar(probs[:, k, 0:n], probs[:, k, 0:n], rden[:, k:k + 1], None,
                                      ALU.mult).then_inc(s_probs, 1)
                    if u + 2 < UNITS:
                        masked(u + 2)
                    if g == G - 1 and not last and s in (0, 2, 6, 10):
                        norm_x((b + 1) * TB, (0, 2, 6, 10).index(s))
                    for kind, t in misc_steps(g, s, last):
                        if kind == "qkt":
                            take_qkt(b * G, g + 1, t)

            every_batch(dve, batch)

            for j in range(TILES // 2):
                for p in range(2):
                    i = j * 2 + p
                    c = [0]

                    def step(ins):
                        c[0] += 1
                        ins.then_inc(s_d1, 1)
                        dve.wait_ge(s_d1, i * 8 + c[0])

                    y = ps[:, p, :]
                    sm = small[:, p, :]
                    dve.wait_ge(s_o, i + 1)
                    step(dve.bn_stats(stats[:, p, :], y))
                    step(dve.bn_aggr(sm[:, 0:2], stats[:, p, :]))
                    dve.tensor_scalar(sm[:, 1:2], sm[:, 1:2], EPS, None, ALU.add).then_inc(s_var, 1)
                    dve.wait_ge(s_sq, i * 2 + 1)
                    step(dve.reciprocal(sm[:, 3:4], sm[:, 2:3]))
                    step(dve.tensor_scalar(delta[:, p, :], y, sm[:, 0:1], sm[:, 3:4], ALU.subtract, ALU.mult))
                    step(dve.tensor_tensor(out=x_sb[:, i, :], in0=x_sb[:, i, :], in1=delta[:, p, :], op=ALU.add))
                    step(dve.bn_stats(stats[:, p, :], x_sb[:, i, :]))
                    step(dve.bn_aggr(sm[:, 4:6], stats[:, p, :]))
                    dve.tensor_scalar(sm[:, 5:6], sm[:, 5:6], EPS, None, ALU.add).then_inc(s_var, 1)
                    dve.wait_ge(s_sq, i * 2 + 2)
                    step(dve.reciprocal(sm[:, 7:8], sm[:, 6:7]))
                    dve.tensor_scalar(x2[:, p, :], x_sb[:, i, :], sm[:, 4:5], sm[:, 7:8],
                                      ALU.subtract, ALU.mult).then_inc(s_x2, 1)
                    dve.wait_ge(s_log_ps, i + 1)
                    dve.tensor_copy(logits[:, i, :], ps[:, 4 + p, 0:E + 1]).then_inc(s_log, 1)
            dve.wait_ge(s_log, TILES)

            c = [0]

            def step(ins):
                c[0] += 1
                ins.then_inc(s_comb2, 1)
                dve.wait_ge(s_comb2, c[0])

            step(dve.tensor_reduce(rt[:, 0, :], logits[:, :, 0:E], AX.X, ALU.max))
            dve.tensor_scalar(rt[:, 0, :], rt[:, 0, :], -1.0, None, ALU.mult).then_inc(s_rd, 1)
            dve.wait_ge(s_re, TILES + 1)
            step(dve.reciprocal(rt[:, 2, :], rt[:, 1, :]))
            bc = lambda a: a.rearrange("p (t o) -> p t o", o=1).broadcast_to([P, TILES, E])
            step(dve.tensor_tensor(out=prob_e, in0=prob_e, in1=bc(rt[:, 2, :]), op=ALU.mult))
            for i in range(TILES):
                dve.max(top[:, i, :], prob_e[:, i, :]).then_inc(s_comb2, 1)
            c[0] += TILES
            dve.wait_ge(s_comb2, c[0])
            for i in range(TILES):
                dve.match_replace(prob_r[:, i, :], top[:, i, :], prob_e[:, i, :], 0.0).then_inc(s_comb2, 1)
            c[0] += TILES
            dve.wait_ge(s_comb2, c[0])
            step(dve.tensor_reduce(rt[:, 3, :], top[:, :, :], AX.X, ALU.add))
            step(dve.reciprocal(rt[:, 3, :], rt[:, 3, :]))
            step(dve.tensor_tensor(out=prob_e, in0=prob_e, in1=prob_r, op=ALU.subtract))
            step(dve.tensor_tensor(out=comb[:, :, 0:E], in0=prob_e, in1=bc(rt[:, 3, :]), op=ALU.mult))
            step(dve.tensor_scalar(rt[:, 4, :], rt[:, 4, :], 1.0, None, ALU.add))
            step(dve.reciprocal(comb[:, :, E], rt[:, 4, :]))
            dve.memset(acc, 0.0).then_inc(s_acc, 1)
            dve.wait_ge(s_acc, 1)

            def expert_dve(e):
                def hid(n):
                    dve.wait_ge(s_silu, e * B + (n + 1))
                    dve.tensor_tensor(out=hidden[:, n % 2, :], in0=gate[:, n % 2, :], in1=ps[:, 2 + n % 2, :],
                                      op=ALU.mult).then_inc(s_hid, 1)
                hid(0)
                for n in range(B):
                    if n + 1 < B:
                        hid(n + 1)
                    for t in range(TB):
                        k = n * TB + t
                        dve.wait_ge(s_down, e * TILES + (k + 1))
                        dve.wait_ge(s_acc, e * TILES + 1) if k == 0 else None
                        dve.scalar_tensor_tensor(out=acc[:, k, :], in0=ps[:, 4 + k % 4, :], scalar=comb[:, k, bass.ts(e, 1)],
                                                 in1=acc[:, k, :], op0=ALU.mult, op1=ALU.add).then_inc(s_acc, 1)

            with dve.Fori(0, EX) as e:
                expert_dve(e)

            dve.wait_ge(s_acc, EX * TILES + 1)
            for i in range(TILES):
                dve.bn_stats(stats[:, i, :], acc[:, i, :]).then_inc(s_fin2, 1)
            dve.wait_ge(s_fin2, TILES)
            for i in range(TILES):
                dve.bn_aggr(moments[:, i, :], stats[:, i, :]).then_inc(s_fin2, 1)
            dve.wait_ge(s_fin2, 2 * TILES)
            dve.tensor_scalar(moments[:, :, 1], moments[:, :, 1], EPS, None, ALU.add).then_inc(s_fd, 1)
            dve.wait_ge(s_fs, 1)
            dve.reciprocal(rstd[:, :], rstd[:, :]).then_inc(s_fd, 1)
            dve.wait_ge(s_fd, 2)
            for i in range(TILES):
                dve.tensor_scalar(acc[:, i, :], acc[:, i, :], moments[:, i, 0:1], rstd[:, i:i + 1],
                                  ALU.subtract, ALU.mult).then_inc(s_fin2, 1)
                dve.wait_ge(s_fin2, 2 * TILES + i + 1)
                dve.tensor_tensor(out=x_sb[:, i, :], in0=x_sb[:, i, :], in1=acc[:, i, :], op=ALU.add).then_inc(s_fin, 1)


def _constants():
    idx = np.arange(0, DH, 2, dtype=np.float32)
    inv_freq = (np.float32(THETA) ** (-idx / np.float32(DH))).astype(np.float32)
    angles = np.arange(S, dtype=np.float32)[:, None] * inv_freq[None, :]
    cos, sin = np.cos(angles).astype(np.float32), np.sin(angles).astype(np.float32)
    rope = np.concatenate([np.repeat(cos, 2, axis=1), -sin, sin], axis=1)
    rope = np.ascontiguousarray(rope.reshape(TB, P, 2 * DH).transpose(1, 0, 2))
    mask = np.zeros((P, S), np.float32)
    mask[:, S - P:] = np.where(np.arange(P)[None, :] > np.arange(P)[:, None], MASKED, 0.0)
    headmask = (np.arange(P)[:, None] // DH == np.arange(HG)[None, :]).astype(np.float32)
    return rope, mask, headmask, np.eye(P, dtype=np.float32)


def kernel(L0_attn_x, L0_attn_Wq, L0_attn_Wk, L0_attn_Wv, L0_attn_Wo, L0_ffn_router_w, L0_ffn_Wg, L0_ffn_Wu,
           L0_ffn_Wd, L0_ffn_Wsg, L0_ffn_Wsu, L0_ffn_Wsd, L0_ffn_Wse):
    import concourse.bacc as bacc
    from concourse.bass_utils import run_bass_kernel_spmd

    def chunks(w):
        w = np.asarray(w)
        return w.T.reshape(-1, P, w.shape[0]).transpose(1, 0, 2)

    qkv = np.stack([chunks(w).reshape(P, DC, G, P) for w in (L0_attn_Wq, L0_attn_Wk, L0_attn_Wv)], axis=3)
    wg = np.concatenate([np.asarray(L0_ffn_Wg), np.asarray(L0_ffn_Wsg)[None]])
    wu = np.concatenate([np.asarray(L0_ffn_Wu), np.asarray(L0_ffn_Wsu)[None]])
    wd = np.concatenate([np.asarray(L0_ffn_Wd), np.asarray(L0_ffn_Wsd)[None]])
    up = np.concatenate([wg, wu], axis=1).transpose(0, 2, 1).reshape(E + 1, DC, P, GATEUP).transpose(0, 2, 1, 3)
    experts = np.concatenate([up.reshape(E + 1, P, DC * GATEUP), wd.transpose(0, 2, 1)], axis=2)
    rope, mask, headmask, ident = _constants()
    arrays = {
        "x": np.asarray(L0_attn_x).reshape(B * S, D),
        "wqkv": qkv.reshape(P, DC, G, QKV),
        "wo": chunks(L0_attn_Wo),
        "router": chunks(np.concatenate([np.asarray(L0_ffn_router_w), np.asarray(L0_ffn_Wse)])),
        "experts": experts,
        "rope": rope, "mask": mask, "headmask": headmask, "ident": ident,
    }
    arrays = {n: np.ascontiguousarray(a) for n, a in arrays.items()}
    nc = bacc.Bacc("TRN2", target_bir_lowering=False, num_devices=1)
    args = [nc.dram_tensor(n, a.shape, mybir.dt.from_np(a.dtype), kind="ExternalInput").ap() for n, a in arrays.items()]
    out = nc.dram_tensor("out", (B * S, D), FP32, kind="ExternalOutput").ap()
    sandwich_kernel(nc, *args, out)
    r = run_bass_kernel_spmd(nc, [arrays], core_ids=[0])
    return r.results[0]["out"].reshape(B, S, D)
```

```python
from contextlib import ExitStack

import numpy as np

import concourse.bass as bass
from concourse import mybir

FP32 = mybir.dt.float32
FP16 = mybir.dt.float16
INT32 = mybir.dt.int32
ACT = mybir.ActivationFunctionType
ALU = mybir.AluOpType
AX = mybir.AxisListType

P = 128
B, S, D = 4, 512, 512
H, DH = 16, 32
E, K, F = 64, 8, 128
THETA = 10000.0
EPS = 1e-5
TB = S // P
TILES = B * TB
DC = D // P
HG = P // DH
G = H // HG
QKV = 3 * P
UNITS = H * TB
GU = UNITS // G
GATEUP = 2 * F
MASKED = -1.0e38
SCALE = float(DH) ** -0.5
WCOLS = DC * GATEUP + D
NW = 8
XROW = D + E
HIGH = (B * S * K + E * (P - 1)) // P + 1
RING = 8


def misc_steps(g, s, last):
    if g < G - 1:
        return [(k, t) for t in range(TB) for k, at in (("proj", 3 * t), ("qkt", 3 * t + 2)) if at == s]
    if last:
        return []
    return [(k, t) for t in range(TB) for k, at in (("xt", 4 * t), ("proj", 4 * t + 1), ("qkt", 4 * t + 3)) if at == s]


def sandwich_kernel(nc, x, wqkv, wo, router, experts, rope, mask, headmask, ident, before, ones, upto, below,
                    steps, count, token, out):
    ctx = ExitStack()
    with ctx:
        def sb(name, shape, dtype=FP32):
            return ctx.enter_context(nc.sbuf_tensor(name, shape, dtype))

        def sem(name):
            return ctx.enter_context(nc.semaphore(name))

        x_sb = sb("x_sb", [P, TILES, D])
        attn_t = sb("attn_t", [P, TILES, G, P])
        x2_t = sb("x2_t", [P, DC, B * S])
        wo_sb = sb("wo_sb", [P, G, D])
        router_sb = sb("router_sb", [P, DC, E + 1])
        rope_sb = sb("rope_sb", [P, TB, 2 * DH])
        mask_sb = sb("mask_sb", [P, S])
        hmask_sb = sb("hmask_sb", [P, HG])
        ident_sb = sb("ident_sb", [P, P])
        before_sb = sb("before_sb", [P, P])
        ones_sb = sb("ones_sb", [P, P])
        upto_sb = sb("upto_sb", [E, E])
        below_sb = sb("below_sb", [E, E])
        steps_sb = sb("steps_sb", [E, TB * B])
        count_sb = sb("count_sb", [P, HIGH])
        token_sb = sb("token_sb", [P, TILES])
        logits = sb("logits", [P, TILES, E + 1])
        stats = sb("stats", [P, TILES, 6])
        moments = sb("moments", [P, TILES, 2])
        rstd = sb("rstd", [P, TILES])
        small = sb("small", [P, 4, 8])
        top = sb("top", [P, TILES, K])
        rt = sb("rt", [P, 5, TILES])
        slot_i = sb("slot_i", [P, TILES, K], INT32)
        part_i = sb("part_i", [P, 2, TILES, K], INT32)
        low_1 = sb("low_1", [P, RING, P], FP16)
        high_1 = sb("high_1", [P, RING, HIGH], FP16)
        n_col = sb("n_col", [E, 4])
        n_cmp = sb("n_cmp", [E, TILES])
        ends_i = sb("ends_i", [1, E], INT32)
        pairs_i = sb("pairs_i", [1, 2], INT32)
        weights_i = sb("weights_i", [1, HIGH], INT32)
        ring_i = sb("ring_i", [1, HIGH], INT32)
        col_i = sb("col_i", [1, HIGH], INT32)
        token_i = sb("token_i", [P, HIGH + 2], INT32)
        idx = sb("idx", [P, 2, 2], INT32)

        big = sb("big", [P, NW * WCOLS])
        wqkv_sb = big[:, 0:DC * G * QKV].rearrange("p (c g n) -> p c g n", c=DC, g=G)
        x_t = big[:, 6144:8192].rearrange("p (c n) -> p c n", c=DC)
        q_pad = big[:, 8192:12288].rearrange("p (a h n) -> p a h n", a=2, h=HG)
        w_ring = big[:, :].rearrange("p (r n) -> p r n", r=NW)

        work = sb("work", [P, 5120])
        probs = work[:, 0:2048].rearrange("p (a n) -> p a n", a=4)
        k_t = work[:, 2048:3072].rearrange("p (a n) -> p a n", a=2)
        roped = work[:, 3072:3584].rearrange("p (a n) -> p a n", a=2)
        rope_cos = work[:, 3584:3840]
        rope_sin = work[:, 3840:4096]
        xn = work[:, 4096:5120].rearrange("p (a n) -> p a n", a=2)
        delta = work[:, 2048:3072].rearrange("p (a n) -> p a n", a=2)
        rows = work[:, 0:2 * XROW].rearrange("p (a n) -> p a n", a=2)
        rows_t = work[:, 1152:2176].rearrange("p (a c n) -> p a c n", a=2, c=DC)
        y_sb = work[:, 2176:3200].rearrange("p (a n) -> p a n", a=2)
        gate = work[:, 3200:3456].rearrange("p (a n) -> p a n", a=2)
        hidden = work[:, 3456:3712].rearrange("p (a n) -> p a n", a=2)
        hidden_t = work[:, 3712:3968].rearrange("p (a n) -> p a n", a=2)
        up_s = work[:, 2176:2432].rearrange("p (a n) -> p a n", a=2)

        qkv_all = sb("qkv_all", [P, 2 * TB * QKV])
        qkv = qkv_all[:, :].rearrange("p (a t n) -> p a t n", a=2, t=TB)
        chosen = qkv_all[:, 0:1024].rearrange("p (t e) -> p t e", e=E)
        earlier = qkv_all[:, 1024:2048 + E].rearrange("p (t e) -> p t e", e=E)
        table_f = qkv_all[:, 2112:2112 + HIGH]
        table_z = qkv_all[:, 2112 + HIGH:2112 + 2 * HIGH]
        slot_f = work[:, 0:P].rearrange("p (t k) -> p t k", k=K)
        part_f = work[:, P:3 * P].rearrange("p (a t k) -> p a t k", a=2, k=K)
        n_rep = qkv_all[0:E, 2496:2496 + P]
        past_end = qkv_all[0:E, 2624:2624 + HIGH]

        prob_e = wo_sb[:, 0:2, :].rearrange("p a n -> p (a n)").rearrange("p (t e) -> p t e", e=E)
        prob_r = wo_sb[:, 2:4, :].rearrange("p a n -> p (a n)").rearrange("p (t e) -> p t e", e=E)
        slots = prob_r
        probs_t = x2_t[:, :, :].rearrange("p c n -> p (c n)")[:, 0:2 * TB * S].rearrange("p (a k n) -> p a k n", a=2, k=TB)
        zeros = x2_t[:, 2:4, :]
        sums = x2_t[:, :, :].rearrange("p c n -> p (c n)").rearrange("p (a s t n) -> p a s t n", a=2, s=2, t=TB)
        y_shared = attn_t[:, :, :, :].rearrange("p t g n -> p t (g n)")

        neg_max = sb("neg_max", [P, 4])
        den = sb("den", [P, 4])
        rden = sb("rden", [P, 4])

        x2_rows = nc.dram_tensor("x2_rows", (B * S, XROW), FP32).ap()
        sum_rows = [nc.dram_tensor(f"sum_rows{p}", (B * S, D), FP32).ap() for p in range(2)]

        ps = ctx.enter_context(nc.psum_tensor("ps", [P, 8, 512], FP32))
        s_bank = [ps[:, i, :] for i in range(4)]
        pt_bank = [ps[:, 4 + i, :] for i in range(2)]
        av_bank = ps[:, 6, :]
        misc = ps[:, 7, :]

        NIN = 14
        s_in = [sem(f"s_in{i}") for i in range(NIN)]
        s_xin = [sem(f"s_xin{i}") for i in range(B)]
        s_moments = sem("s_moments")
        s_ln = sem("s_ln")
        s_std = sem("s_std")
        s_xn = sem("s_xn")
        s_xt_ps = sem("s_xt_ps")
        s_xt = sem("s_xt")
        s_qkv_ps = sem("s_qkv_ps")
        s_qkv = sem("s_qkv")
        s_rtmp = sem("s_rtmp")
        s_rope = sem("s_rope")
        s_qkt_ps = sem("s_qkt_ps")
        s_qkt = sem("s_qkt")
        s_scored = sem("s_scored")
        s_masked = sem("s_masked")
        s_exp = sem("s_exp")
        s_recip = sem("s_recip")
        s_probs = sem("s_probs")
        s_turned = sem("s_turned")
        s_pt = sem("s_pt")
        s_av = sem("s_av")
        s_attn = sem("s_attn")
        s_own = sem("s_own")
        s_y_ps = sem("s_y_ps")
        s_var = sem("s_var")
        s_sq = sem("s_sq")
        s_stat = sem("s_stat")
        s_x2 = sem("s_x2")
        s_x2t_ps = sem("s_x2t_ps")
        s_x2t = sem("s_x2t")
        s_log_ps = sem("s_log_ps")
        s_log = sem("s_log")
        s_zero = sem("s_zero")
        s_neg = sem("s_neg")
        s_e1 = sem("s_e1")
        s_route = sem("s_route")
        s_comb = sem("s_comb")
        s_cnt_ps = sem("s_cnt_ps")
        s_cnt = sem("s_cnt")
        s_ends_ps = sem("s_ends_ps")
        s_slots_ps = sem("s_slots_ps")
        s_slots = sem("s_slots")
        s_row_ps = sem("s_row_ps")
        s_tables = sem("s_tables")
        s_high = sem("s_high")
        s_one_used = sem("s_one_used")
        s_table_ps = sem("s_table_ps")
        s_table = sem("s_table")
        s_sgu = sem("s_sgu")
        s_silu = sem("s_silu")
        s_up = sem("s_up")
        s_shid = sem("s_shid")
        s_sht = sem("s_sht")
        s_shte = sem("s_shte")
        s_sdn = sem("s_sdn")
        s_sy = sem("s_sy")
        s_ready = sem("s_ready")
        s_idx = sem("s_idx")
        s_weight = sem("s_weight")
        s_issue = sem("s_issue")
        s_xg_ps = sem("s_xg_ps")
        s_xg = sem("s_xg")
        s_gu = sem("s_gu")
        s_gate = sem("s_gate")
        s_hid = sem("s_hid")
        s_ht_ps = sem("s_ht_ps")
        s_ht = sem("s_ht")
        s_dn = sem("s_dn")
        s_y = sem("s_y")
        s_sum = sem("s_sum")
        s_lnb = sem("s_lnb")
        s_lnf = sem("s_lnf")
        s_lnd = sem("s_lnd")
        s_norm = sem("s_norm")
        s_fin = sem("s_fin")
        s_out = sem("s_out")
        s_x2d = [sem(f"s_x2d{p}") for p in range(2)]
        s_tok = sem("s_tok")
        s_combd = sem("s_combd")
        s_wl = [sem(f"s_wl{r}") for r in range(NW)]
        s_ws = sem("s_ws")
        s_gather = [sem(f"s_gather{p}") for p in range(2)]
        s_scatter = [sem(f"s_scatter{p}") for p in range(2)]
        s_sums = [sem(f"s_sums{p}") for p in range(4)]

        block = ctx.enter_context(nc.Block())
        x_v = x.rearrange("(t p) d -> p t d", p=P)
        out_v = out.rearrange("(t p) d -> p t d", p=P)

        sums_v = [r.rearrange("(t p) d -> p t d", p=P) for r in sum_rows]
        x2_v = x2_rows.rearrange("(t p) d -> p t d", p=P)
        LOADS = [(ident_sb[:, :], ident), (rope_sb[:, :, :], rope), (hmask_sb[:, :], headmask),
                 (mask_sb[:, :], mask), (wo_sb[:, :, :], wo), (router_sb[:, :, :], router),
                 (before_sb[:, :], before), (ones_sb[:, :], ones), (upto_sb[:, :], upto), (below_sb[:, :], below),
                 (steps_sb[:, :], steps), (count_sb[:, :], count), (token_sb[:, :], token)]
        I_IDENT, I_ROPE, I_HMASK, I_MASK, I_WO, I_ROUTER, I_BEFORE, I_ONES, I_UPTO, I_BELOW, I_STEPS, I_COUNT, I_TOKEN, I_WQKV = range(14)


        def every_batch(eng, body):
            with eng.Fori(0, B - 1) as b:
                body(b, False)
            body(B - 1, True)

        @block.sync
        def _(sp):
            sp.dma_start(x_sb[:, 0:TB, :], x_v[:, 0:TB, :]).then_inc(s_xin[0], 16)
            sp.dma_start(ident_sb[:, :], ident).then_inc(s_in[I_IDENT], 16)
            sp.dma_start(wqkv_sb[:, :, :, :], wqkv).then_inc(s_in[I_WQKV], 16)
            for i in range(1, len(LOADS)):
                sp.dma_start(*LOADS[i]).then_inc(s_in[i], 16)
            for b in range(1, B):
                sp.dma_start(x_sb[:, b * TB:(b + 1) * TB, :], x_v[:, b * TB:(b + 1) * TB, :]).then_inc(s_xin[b], 16)
            sp.wait_ge(s_attn, B * G)
            for r in range(NW - 1):
                sp.dma_start(w_ring[:, r, :], experts[r]).then_inc(s_wl[r], 16)
            sp.dma_start(w_ring[:, NW - 1, :], experts[E]).then_inc(s_ws, 16)
            for i in range(TILES):
                sp.wait_ge(s_x2, i + 1)
                sp.dma_start(x2_v[:, i, 0:D], xn[:, i % 2, :]).then_inc(s_x2d[i % 2], 16)
            sp.wait_ge(s_comb, 1)
            with nc.allow_non_contiguous_dma(reason="64 weights beside each row"):
                sp.dma_start(x2_v[:, :, D:XROW], prob_e).then_inc(s_combd, 16)
            sp.wait_ge(s_sdn, TILES)
            sp.dma_start(w_ring[:, NW - 1, :], experts[NW - 1]).then_inc(s_wl[NW - 1], 16)
            for r in range(NW):
                sp.wait_ge(s_wl[r], 16)
                sp.sem_inc(s_ready, 1)
            sp.wait_ge(s_tables, 4)
            with sp.Fori(0, E // NW - 1) as j:
                for r in range(NW):
                    end = sp.value_load(ends_i[0:1, bass.ts(j * NW + r, 1)], min_val=1, max_val=HIGH)
                    sp.wait_ge(s_dn, end)
                    sp.dma_start(w_ring[:, r, :], experts[j * NW + (r + NW)]).then_inc(s_wl[r], 16)
                    if r >= 2:
                        sp.wait_ge(s_wl[r - 2], (j + 2) * 16)
                        sp.sem_inc(s_ready, 1)
                for r in range(NW - 2, NW):
                    sp.wait_ge(s_wl[r], (j + 2) * 16)
                    sp.sem_inc(s_ready, 1)
            pairs = sp.value_load(pairs_i[0:1, 1:2], min_val=HIGH // 2 - TILES * 2, max_val=HIGH // 2 - 1)
            for p in range(2):
                sp.wait_ge(s_scatter[p], (pairs + (3 - p)) * 16)
            for b in range(B):
                if b >= 2:
                    sp.wait_ge(s_sum, (b - 1) * TB)
                for p in range(2):
                    sp.dma_start(sums[:, b % 2, p, :, :], sums_v[p][:, b * TB:(b + 1) * TB, :]).then_inc(s_sums[b], 16)
            for i in range(TILES):
                sp.wait_ge(s_fin, i + 1)
                sp.dma_start(out_v[:, i, :], x_sb[:, i, :]).then_inc(s_out, 16)
            sp.wait_ge(s_out, 16 * TILES)

        @block.gpsimd
        def _(pool):
            def rope_group_tile(i4, g, t):
                n = (i4 + g) * TB + t
                src = qkv[:, g % 2, t, 0:2 * P]
                pair = src.rearrange("p (h j e) -> p h j e", h=2 * HG, e=2)
                sin_pair = rope_sin[:, :].rearrange("p (h j e) -> p h j e", h=2 * HG, e=2)
                heads = src.rearrange("p (h d) -> p h d", h=2 * HG)
                cos = rope_sb[:, t, 0:DH].rearrange("p (o d) -> p o d", o=1).broadcast_to([P, 2 * HG, DH])
                nsin = rope_sb[:, t, DH:DH + 16].rearrange("p (o d) -> p o d", o=1).broadcast_to([P, 2 * HG, 16])
                psin = rope_sb[:, t, DH + 16:DH + 32].rearrange("p (o d) -> p o d", o=1).broadcast_to([P, 2 * HG, 16])
                pool.wait_ge(s_qkv, n + 1)
                pool.tensor_tensor(out=rope_cos[:, :].rearrange("p (h d) -> p h d", h=2 * HG), in0=heads,
                                   in1=cos, op=ALU.mult).then_inc(s_rtmp, 1)
                pool.tensor_tensor(out=sin_pair[:, :, :, 0], in0=pair[:, :, :, 1], in1=nsin,
                                   op=ALU.mult).then_inc(s_rtmp, 1)
                pool.tensor_tensor(out=sin_pair[:, :, :, 1], in0=pair[:, :, :, 0], in1=psin,
                                   op=ALU.mult).then_inc(s_rtmp, 1)
                pool.wait_ge(s_rtmp, (n + 1) * 3)
                pool.tensor_tensor(out=roped[:, t % 2, :], in0=rope_cos[:, :], in1=rope_sin[:, :],
                                   op=ALU.add).then_inc(s_rope, 1)
                pool.wait_ge(s_rope, n + 1)

            pool.memset(zeros, 0.0).then_inc(s_zero, 1)
            pool.wait_ge(s_zero, 1)
            for p in range(2):
                for half in range(2):
                    pool.dma_start(sums_v[p][:, 8 * half:8 * half + 8, :],
                                   zeros.rearrange("p c n -> p (c n)").rearrange("p (t n) -> p t n", n=D)).then_inc(s_scatter[p], 16)
            pool.wait_ge(s_in[I_ROPE], 16)
            for t in range(TB):
                rope_group_tile(0, 0, t)

            def batch(b, last):
                for g in range(1, G + (not last)):
                    for t in range(TB):
                        rope_group_tile(b * G, g, t)

            every_batch(pool, batch)

            for i in range(TILES):
                pool.wait_ge(s_up, i + 1)
                if i >= 2:
                    pool.wait_ge(s_sht, i - 1)
                pool.tensor_tensor(out=hidden[:, i % 2, :], in0=gate[:, i % 2, :], in1=up_s[:, i % 2, :],
                                   op=ALU.mult).then_inc(s_shid, 1)

            def gather(p):
                pool.indirect_dma_start(rows[:, p, :], None, x2_rows,
                                        bass.IndirectOffsetOnAxis(ap=idx[:, p, 0:1], axis=0)).then_inc(s_gather[p], 16)

            def scatter(p):
                pool.indirect_dma_start(sum_rows[p], bass.IndirectOffsetOnAxis(ap=idx[:, p, 1:2], axis=0), y_sb[:, p, :],
                                        None, bounds_check=last_row, oob_is_err=False,
                                        compute_op=ALU.add).then_inc(s_scatter[p], 16)

            last_row = pool.to_reg(B * S - 1)
            for p in range(2):
                pool.wait_ge(s_x2d[p], 16 * (TILES // 2))
            pool.wait_ge(s_combd, 16)
            pool.wait_ge(s_sht, TILES)
            pool.wait_ge(s_shte, TILES)
            pool.wait_ge(s_tables, 4)
            pairs = pool.value_load(pairs_i[0:1, 1:2], min_val=HIGH // 2 - TILES * 2, max_val=HIGH // 2 - 1)
            for t in range(4):
                pool.wait_ge(s_idx, t + 1)
                if t >= 2:
                    pool.wait_ge(s_xg_ps, t - 1)
                    pool.wait_ge(s_weight, t - 1)
                gather(t % 2)
            with pool.Fori(0, pairs) as j:
                for p in range(2):
                    t = j * 2 + (p + 2)
                    pool.wait_ge(s_idx, t + 3)
                    pool.wait_ge(s_xg_ps, t + 1)
                    pool.wait_ge(s_weight, t + 1)
                    pool.sem_inc(s_issue, 1)
                    gather(p)
                    pool.wait_ge(s_y, t - 1)
                    pool.sem_inc(s_issue, 1)
                    scatter(p)
            pool.wait_ge(s_y, pairs * 2 + 1)
            pool.sem_inc(s_issue, 1)
            scatter(0)
            for p in range(2):
                pool.wait_ge(s_gather[p], (pairs + 2) * 16)
            for i in range(TILES):
                pool.wait_ge(s_norm, i + 1)
                pool.tensor_tensor(out=x_sb[:, i, :], in0=x_sb[:, i, :], in1=y_shared[:, i, :],
                                   op=ALU.add).then_inc(s_fin, 1)

        @block.scalar
        def _(act):
            act.wait_ge(s_ln, 1)
            act.activation(rstd[:, :], moments[:, :, 1], ACT.Sqrt).then_inc(s_std, 1)

            def evac_xt(b4, t):
                act.wait_ge(s_xt_ps, b4 + t + 1)
                act.activation(x_t[:, :, bass.ts(t, P)], misc.rearrange("p (c n) -> p c n", c=DC),
                               ACT.Copy).then_inc(s_xt, 1)

            def evac_qkv(i4, g, t):
                n = (i4 + g) * TB + t
                act.wait_ge(s_qkv_ps, n + 1)
                act.activation(qkv[:, g % 2, t, :], misc[:, 0:QKV], ACT.Copy).then_inc(s_qkv, 1)

            for t in range(TB):
                evac_xt(0, t)
                evac_qkv(0, 0, t)

            def exp(b, u):
                act.wait_ge(s_masked, b * UNITS + (u + 1))
                n = (u % TB + 1) * P
                act.activation(probs[:, u % 4, 0:n], s_bank[u % 4][:, 0:n], ACT.Exp, bias=neg_max[:, u % 4:u % 4 + 1],
                               scale=-1.0, accum_out=den[:, u % 4:u % 4 + 1]).then_inc(s_exp, 1)

            def evac_pt(b, u):
                h, qt = divmod(u, TB)
                act.wait_ge(s_turned, b * UNITS + (u + 1))
                if h >= 2 and qt == 0:
                    act.wait_ge(s_av, b * H + (h - 1))
                act.activation(probs_t[:, h % 2, 0:qt + 1, bass.ts(qt, P)],
                               pt_bank[u % 2].rearrange("p (k n) -> p k n", k=TB)[:, 0:qt + 1, :],
                               ACT.Copy).then_inc(s_pt, 1)

            def evac_attn(b, g):
                act.wait_ge(s_av, b * H + HG * (g + 1))
                act.activation(attn_t[:, bass.ts(b, TB), g, :],
                               av_bank.rearrange("p (t n) -> p t n", t=TB), ACT.Copy).then_inc(s_attn, 1)

            def batch(b, last):
                exp(b, 0)
                exp(b, 1)
                for u in range(UNITS):
                    g, s = divmod(u, GU)
                    if u >= 1:
                        evac_pt(b, u - 1)
                    if u + 2 < UNITS:
                        exp(b, u + 2)
                    if s == 1 and g >= 1:
                        evac_attn(b, g - 1)
                    for kind, t in misc_steps(g, s, last):
                        if kind == "xt":
                            evac_xt((b + 1) * TB, t)
                        if kind == "proj":
                            evac_qkv(b * G, g + 1, t)
                evac_pt(b, UNITS - 1)
                evac_attn(b, G - 1)

            every_batch(act, batch)

            for i in range(TILES + 2):
                if i < TILES:
                    act.wait_ge(s_var, max(2 * i, 1))
                    act.activation(small[:, i % 4, 2:3], small[:, i % 4, 1:2], ACT.Sqrt).then_inc(s_sq, 1)
                if 1 <= i <= TILES:
                    act.wait_ge(s_var, min(2 * i + 1, 2 * TILES))
                    act.activation(small[:, (i - 1) % 4, 6:7], small[:, (i - 1) % 4, 5:6], ACT.Sqrt).then_inc(s_sq, 1)
                if i == 2:
                    for p in range(2):
                        act.wait_ge(s_scatter[p], 32)
                if i >= 2:
                    k = i - 2
                    act.wait_ge(s_x2t_ps, k + 1)
                    act.activation(x2_t[:, :, bass.ts(k, P)], ps[:, 2 + k % 2, :].rearrange("p (c n) -> p c n", c=DC),
                                   ACT.Copy).then_inc(s_x2t, 1)
            act.wait_ge(s_neg, 1)
            for i in range(TILES):
                act.activation(prob_e[:, i, :], logits[:, i, 0:E], ACT.Exp, bias=rt[:, 0, i:i + 1],
                               accum_out=rt[:, 1, i:i + 1]).then_inc(s_e1, 1)
            act.activation(rt[:, 4, :], logits[:, :, E], ACT.Exp, scale=-1.0).then_inc(s_e1, 1)

            for i in range(TILES + 1):
                if i < TILES:
                    act.wait_ge(s_sgu, i + 1)
                    if i >= 2:
                        act.wait_ge(s_shid, i - 1)
                    act.activation(gate[:, i % 2, :], ps[:, 2 + i % 2, 0:F], ACT.Silu).then_inc(s_silu, 1)
                    act.activation(up_s[:, i % 2, :], ps[:, 2 + i % 2, F:GATEUP], ACT.Copy).then_inc(s_up, 1)
                if i >= 1:
                    k = i - 1
                    act.wait_ge(s_sht, k + 1)
                    act.activation(hidden_t[:, k % 2, :], ps[:, 4, 0:P], ACT.Copy).then_inc(s_shte, 1)
                    act.wait_ge(s_sdn, k + 1)
                    act.activation(y_shared[:, k, :], ps[:, 5, :], ACT.Copy).then_inc(s_sy, 1)

            act.wait_ge(s_tables, 4)
            pairs = act.value_load(pairs_i[0:1, 1:2], min_val=HIGH // 2 - TILES * 2, max_val=HIGH // 2 - 1)

            def turned(t, p):
                act.wait_ge(s_xg_ps, t + 1)
                act.activation(rows_t[:, p, :, :], ps[:, p, :].rearrange("p (c n) -> p c n", c=DC),
                               ACT.Copy).then_inc(s_xg, 1)

            def silu(t, p):
                act.wait_ge(s_gu, t + 1)
                act.activation(gate[:, p, :], ps[:, 2 + p, 0:F], ACT.Silu).then_inc(s_gate, 1)

            turned(0, 0)
            silu(0, 0)
            turned(1, 1)
            with act.Fori(0, pairs) as j:
                for p in range(2):
                    t = j * 2 + (p + 1)
                    silu(t, (p + 1) % 2)
                    turned(t + 1, p)
            act.preload_act_table(ACT.Sqrt)
            for b in range(B):
                act.wait_ge(s_lnb, b + 1)
                act.activation(rstd[:, bass.ts(b, TB)], moments[:, bass.ts(b, TB), 1], ACT.Sqrt).then_inc(s_lnf, 1)

        @block.tensor
        def _(pe):
            def xt(b4, t, first=False):
                pe.wait_ge(s_xn, b4 + t + 1)
                if not (first and t == 0):
                    pe.wait_ge(s_qkt, b4 * G + t)
                for c in range(DC):
                    mm = pe.transpose(misc[:, bass.ts(c, P)], xn[:, t % 2, bass.ts(c, P)], ident_sb[:, :])
                mm.then_inc(s_xt_ps, 1)

            def proj(i4, g, t, after_xt=None):
                if after_xt is not None:
                    pe.wait_ge(s_xt, after_xt + t + 1)
                else:
                    pe.wait_ge(s_qkt, (i4 + g) * TB + t)
                for c in range(DC):
                    mm = pe.matmul(misc[:, 0:QKV], x_t[:, c, bass.ts(t, P)], wqkv_sb[:, c, g % G, :],
                                   start=(c == 0), stop=(c == DC - 1))
                mm.then_inc(s_qkv_ps, 1)

            def qkt(i4, g, t):
                pe.wait_ge(s_rope, (i4 + g) * TB + (t + 1))
                for c in range(2):
                    mm = pe.transpose(misc[:, bass.ts(c, P)], roped[:, t % 2, bass.ts(c, P)], ident_sb[:, :])
                mm.then_inc(s_qkt_ps, 1)

            pe.wait_ge(s_in[I_IDENT], 16)
            for t in range(TB):
                xt(0, t, first=True)
                if t == 0:
                    pe.wait_ge(s_in[I_WQKV], 16)
                proj(0, 0, t, after_xt=0)
                qkt(0, 0, t)

            def score(b, u):
                g, (h, qt) = u // GU, divmod(u % GU, TB)
                pe.wait_ge(s_qkt, (b * G + g) * TB + (qt + 1))
                n = (qt + 1) * P
                pe.matmul(s_bank[u % 4][:, 0:n], q_pad[:, g % 2, h, bass.ts(qt, P)], k_t[:, g % 2, 0:n],
                          start=True, stop=True).then_inc(s_scored, 1)

            def turn(b, u):
                qt = u % TB
                pe.wait_ge(s_probs, b * UNITS + (u + 1))
                if u >= 2:
                    pe.wait_ge(s_pt, b * UNITS + (u - 1))
                for k in range(qt + 1):
                    mm = pe.transpose(pt_bank[u % 2][:, bass.ts(k, P)], probs[:, u % 4, bass.ts(k, P)], ident_sb[:, :])
                mm.then_inc(s_turned, 1)

            def weigh(b, h):
                g, hh = divmod(h, HG)
                pe.wait_ge(s_pt, b * UNITS + TB * (h + 1))
                if hh == 0 and g >= 1:
                    pe.wait_ge(s_attn, b * G + g)
                o = av_bank[DH * hh:DH * (hh + 1), :]
                for k in range(TB):
                    v0 = 2 * P + DH * hh
                    mm = pe.matmul(o[:, k * P:S], qkv[:, g % 2, k, v0:v0 + DH], probs_t[:, h % 2, k, k * P:S],
                                   start=(k == 0), stop=(k == TB - 1))
                mm.then_inc(s_av, 1)

            def batch(b, last):
                pe.wait_ge(s_qkt, (b * G) * TB + TB)
                for u in range(3):
                    score(b, u)
                for u in range(UNITS):
                    g, s = divmod(u, GU)
                    if u + 3 < UNITS:
                        score(b, u + 3)
                    turn(b, u)
                    if u >= TB and u % TB == 0:
                        weigh(b, u // TB - 1)
                    for kind, t in misc_steps(g, s, last):
                        if kind == "xt":
                            xt((b + 1) * TB, t)
                        if kind == "proj":
                            proj(b * G, g + 1, t, after_xt=(b + 1) * TB if g == G - 1 else None)
                        if kind == "qkt":
                            qkt(b * G, g + 1, t)
                weigh(b, H - 1)
                pe.wait_ge(s_attn, b * G + G)

            every_batch(pe, batch)

            pe.wait_ge(s_in[I_WO], 16)
            pe.wait_ge(s_in[I_ROUTER], 16)

            def project(i):
                if i >= 2:
                    pe.wait_ge(s_stat, i - 1)
                for g in range(G):
                    mm = pe.matmul(ps[:, i % 2, :], attn_t[:, i, g, :], wo_sb[:, g, :], start=(g == 0), stop=(g == G - 1))
                mm.then_inc(s_y_ps, 1)

            def turn_x2(i):
                pe.wait_ge(s_x2, i + 1)
                if i >= 2:
                    pe.wait_ge(s_x2t, i - 1)
                for c in range(DC):
                    mm = pe.transpose(ps[:, 2 + i % 2, bass.ts(c, P)], xn[:, i % 2, bass.ts(c, P)], ident_sb[:, :])
                mm.then_inc(s_x2t_ps, 1)

            def route(i):
                pe.wait_ge(s_x2t, i + 1)
                if i >= 2:
                    pe.wait_ge(s_log, i - 1)
                for c in range(DC):
                    mm = pe.matmul(ps[:, 4 + i % 2, 0:E + 1], x2_t[:, c, bass.ts(i, P)], router_sb[:, c, :],
                                   start=(c == 0), stop=(c == DC - 1))
                mm.then_inc(s_log_ps, 1)

            for i in range(TILES + 3):
                if i < TILES:
                    project(i)
                if i >= 3:
                    route(i - 3)
                if 2 <= i < TILES + 2:
                    turn_x2(i - 2)

            def shared_up(i):
                if i >= 2:
                    pe.wait_ge(s_up, i - 1)
                if i == 0:
                    pe.wait_ge(s_ws, 16)
                    pe.wait_ge(s_x2t, TILES)
                for c in range(DC):
                    mm = pe.matmul(ps[:, 2 + i % 2, 0:GATEUP], x2_t[:, c, bass.ts(i, P)],
                                   w_ring[:, NW - 1, c * GATEUP:(c + 1) * GATEUP], start=(c == 0), stop=(c == DC - 1))
                mm.then_inc(s_sgu, 1)

            def shared_turn(i):
                pe.wait_ge(s_shid, i + 1)
                if i >= 1:
                    pe.wait_ge(s_shte, i)
                if i == 0:
                    pe.wait_ge(s_log, TILES)
                pe.transpose(ps[:, 4, 0:P], hidden[:, i % 2, :], ident_sb[:, :]).then_inc(s_sht, 1)

            def shared_down(i):
                pe.wait_ge(s_shte, i + 1)
                if i >= 1:
                    pe.wait_ge(s_sy, i)
                pe.matmul(ps[:, 5, :], hidden_t[:, i % 2, :], w_ring[:, NW - 1, DC * GATEUP:WCOLS],
                          start=True, stop=True).then_inc(s_sdn, 1)

            tables = ps[:, 7, :]

            def count_rows():
                pe.wait_ge(s_route, 1)
                pe.matmul(tables[0:E, 0:1], earlier[:, TILES, :], ones_sb[:, 0:1], start=True, stop=True).then_inc(s_cnt_ps, 1)

            def place_rows():
                pe.wait_ge(s_cnt, 1)
                pe.matmul(tables[0:E, 8:9], upto_sb[:, :], n_col[:, 1:2], start=True, stop=True)
                pe.matmul(tables[0:1, 16:16 + E], n_col[:, 1:2], upto_sb[:, :], start=True, stop=True).then_inc(s_ends_ps, 1)
                for half in range(2):
                    o = ps[:, half, :]
                    mine = chosen[:, 8 * half:8 * half + 8, :].rearrange("p t e -> p (t e)")
                    ahead = earlier[:, 8 * half:8 * half + 8, :].rearrange("p t e -> p (t e)")
                    pe.matmul(o, before_sb[:, :], mine, start=True, stop=False)
                    pe.matmul(o, ones_sb[:, :], ahead, start=False, stop=False)
                    for k in range(8):
                        mm = pe.matmul(o[:, k * E:(k + 1) * E], n_rep, below_sb[:, :], start=False, stop=(k == 7))
                mm.then_inc(s_slots_ps, 1)

            def tile_rows():
                pe.wait_ge(s_cnt, 2)
                pe.matmul(tables[0:1, 96:96 + HIGH], ones_sb[0:E, 0:1], past_end, start=True, stop=True).then_inc(s_row_ps, 1)

            def fill_table(n):
                for m in range(n * K, (n + 1) * K):
                    pe.wait_ge(s_high, m + 1)
                    mm = pe.matmul(ps[:, 6, 0:HIGH], low_1[:, m % RING, :], high_1[:, m % RING, :],
                                   start=(m == 0), stop=(m == TILES * K - 1))
                    mm.then_inc(s_one_used, 1)

            for i in range(TILES + 1):
                if i < TILES:
                    shared_up(i)
                if i >= 1:
                    shared_turn(i - 1)
                    shared_down(i - 1)
                if i == 7:
                    count_rows()
                if i == 8:
                    place_rows()
                if i == 9:
                    tile_rows()
                if i >= 12 and i < TILES:
                    fill_table(i - 12)
            for n in range(4, TILES):
                fill_table(n)

            def turn_rows(t, p, r):
                pe.wait_ge(s_gather[p], r)
                if not isinstance(t, int) or t >= 2:
                    pe.wait_ge(s_xg, t - 1)
                for c in range(DC):
                    mm = pe.transpose(ps[:, p, bass.ts(c, P)], rows[:, p, bass.ts(c, P)], ident_sb[:, :])
                mm.then_inc(s_xg_ps, 1)

            def up(t, p):
                need = pe.value_load(weights_i[0:1, bass.ts(t, 1)], min_val=1, max_val=E)
                slot = pe.value_load(ring_i[0:1, bass.ts(t, 1)], min_val=0, max_val=NW - 1)
                pe.wait_ge(s_ready, need)
                pe.wait_ge(s_xg, t + 1)
                for c in range(DC):
                    mm = pe.matmul(ps[:, 2 + p, 0:GATEUP], rows_t[:, p, c, :], w_ring[:, slot, c * GATEUP:(c + 1) * GATEUP],
                                   start=(c == 0), stop=(c == DC - 1))
                mm.then_inc(s_gu, 1)

            def turn_hidden(t, p):
                pe.wait_ge(s_hid, t + 1)
                pe.transpose(ps[:, 4, 0:P], hidden[:, p, :], ident_sb[:, :]).then_inc(s_ht_ps, 1)

            def down(t, p):
                slot = pe.value_load(ring_i[0:1, bass.ts(t, 1)], min_val=0, max_val=NW - 1)
                pe.wait_ge(s_ht, t + 1)
                pe.matmul(ps[:, 5 + p, :], hidden_t[:, p, :], w_ring[:, slot, DC * GATEUP:WCOLS],
                          start=True, stop=True).then_inc(s_dn, 1)

            pe.wait_ge(s_table, 1)
            pe.sem_inc(s_dn, 1)
            pairs = pe.value_load(pairs_i[0:1, 1:2], min_val=HIGH // 2 - TILES * 2, max_val=HIGH // 2 - 1)
            turn_rows(0, 0, 16)
            up(0, 0)
            turn_rows(1, 1, 16)
            turn_hidden(0, 0)
            with pe.Fori(0, pairs) as j:
                up(j * 2 + 1, 1)
                turn_rows(j * 2 + 2, 0, (j + 2) * 16)
                down(j * 2, 0)
                turn_hidden(j * 2 + 1, 1)
                up(j * 2 + 2, 0)
                turn_rows(j * 2 + 3, 1, (j + 2) * 16)
                down(j * 2 + 1, 1)
                turn_hidden(j * 2 + 2, 0)
            down(pairs * 2, 0)

        @block.vector
        def _(dve):
            for b in range(B):
                dve.wait_ge(s_xin[b], 16)
                for t in range(b * TB, (b + 1) * TB):
                    dve.bn_stats(stats[:, t, :], x_sb[:, t, :]).then_inc(s_moments, 1)
            dve.wait_ge(s_moments, TILES)
            for t in range(TILES):
                dve.bn_aggr(moments[:, t, :], stats[:, t, :]).then_inc(s_moments, 1)
            dve.wait_ge(s_moments, 2 * TILES)
            dve.tensor_scalar(moments[:, :, 1], moments[:, :, 1], EPS, None, ALU.add).then_inc(s_ln, 1)
            dve.wait_ge(s_std, 1)
            dve.reciprocal(rstd[:, :], rstd[:, :]).then_inc(s_ln, 1)
            dve.wait_ge(s_ln, 2)

            def norm_x(b4, t, first=False):
                if not (first and t < 2):
                    dve.wait_ge(s_xt_ps, b4 + t - 1)
                m = b4 + t
                dve.tensor_scalar(xn[:, t % 2, :], _row(x_sb, m),
                                  _col2(moments, m, 0), _col(rstd, m), ALU.subtract, ALU.mult).then_inc(s_xn, 1)

            def _row(t, m):
                return t[:, m, :]

            def _col(t, m):
                return t[:, bass.ts(m, 1)]

            def _col2(t, m, k):
                return t[:, m, k:k + 1]

            def take_qkt(i4, g, t):
                n = (i4 + g) * TB + t
                dve.wait_ge(s_qkt_ps, n + 1)
                dve.tensor_copy(k_t[:, g % 2, bass.ts(t, P)], misc[:, P:2 * P])
                q = misc[:, 0:P].rearrange("p (o n) -> p o n", o=1).broadcast_to([P, HG, P])
                hm = hmask_sb[:, :].rearrange("p (h o) -> p h o", o=1).broadcast_to([P, HG, P])
                dve.tensor_tensor(out=q_pad[:, g % 2, :, bass.ts(t, P)], in0=q, in1=hm, op=ALU.mult).then_inc(s_qkt, 1)

            dve.wait_ge(s_in[I_HMASK], 16)
            for t in range(TB):
                norm_x(0, t, first=True)
                if t >= 1:
                    take_qkt(0, 0, t - 1)
            take_qkt(0, 0, TB - 1)
            dve.wait_ge(s_in[I_MASK], 16)

            def masked(u):
                n = (u % TB + 1) * P
                sc = s_bank[u % 4][:, 0:n]
                dve.tensor_tensor_reduce(sc, sc, mask_sb[:, S - n:S], -SCALE, 3.0e38, ALU.add, ALU.min,
                                         neg_max[:, u % 4:u % 4 + 1]).then_inc(s_masked, 1)

            def batch(b, last):
                dve.wait_ge(s_scored, b * UNITS + 2)
                dve.memset(rden[:, :], 0.0).then_inc(s_recip, 1)
                masked(0)
                masked(1)
                for u in range(UNITS):
                    g, s = divmod(u, GU)
                    k, n = u % 4, (u % TB + 1) * P
                    dve.wait_ge(s_exp, b * UNITS + (u + 1))
                    if u == 0:
                        dve.wait_ge(s_recip, b * (UNITS + 1) + 1)
                    dve.reciprocal(rden[:, k:k + 1], den[:, k:k + 1]).then_inc(s_recip, 1)
                    if u + 2 < UNITS:
                        dve.wait_ge(s_scored, b * UNITS + (u + 3))
                    dve.wait_ge(s_recip, b * (UNITS + 1) + (u + 2))
                    dve.tensor_scalar(probs[:, k, 0:n], probs[:, k, 0:n], rden[:, k:k + 1], None,
                                      ALU.mult).then_inc(s_probs, 1)
                    if u + 2 < UNITS:
                        masked(u + 2)
                    if g == G - 1 and not last and s in (0, 2, 6, 10):
                        norm_x((b + 1) * TB, (0, 2, 6, 10).index(s))
                    for kind, t in misc_steps(g, s, last):
                        if kind == "qkt":
                            take_qkt(b * G, g + 1, t)

            every_batch(dve, batch)

            own = [0]

            def step(ins):
                own[0] += 1
                ins.then_inc(s_own, 1)
                dve.wait_ge(s_own, own[0])

            def attention_moments(i):
                sm = small[:, i % 4, :]
                dve.wait_ge(s_y_ps, i + 1)
                step(dve.bn_stats(stats[:, i, :], ps[:, i % 2, :]))
                step(dve.bn_aggr(sm[:, 0:2], stats[:, i, :]))
                dve.tensor_scalar(sm[:, 1:2], sm[:, 1:2], EPS, None, ALU.add).then_inc(s_var, 1)

            def first_residual(i):
                sm = small[:, i % 4, :]
                dve.wait_ge(s_sq, max(2 * i, 1))
                step(dve.reciprocal(sm[:, 3:4], sm[:, 2:3]))
                dve.tensor_scalar(delta[:, i % 2, :], ps[:, i % 2, :], sm[:, 0:1], sm[:, 3:4],
                                  ALU.subtract, ALU.mult).then_inc(s_stat, 1)
                dve.wait_ge(s_stat, i + 1)
                step(dve.tensor_tensor(out=x_sb[:, i, :], in0=x_sb[:, i, :], in1=delta[:, i % 2, :], op=ALU.add))
                step(dve.bn_stats(stats[:, i, :], x_sb[:, i, :]))
                step(dve.bn_aggr(sm[:, 4:6], stats[:, i, :]))
                dve.tensor_scalar(sm[:, 5:6], sm[:, 5:6], EPS, None, ALU.add).then_inc(s_var, 1)

            def second_norm(i):
                sm = small[:, i % 4, :]
                dve.wait_ge(s_sq, min(2 * i + 3, 2 * TILES))
                step(dve.reciprocal(sm[:, 7:8], sm[:, 6:7]))
                if i >= 2:
                    dve.wait_ge(s_x2d[i % 2], 16 * (i // 2))
                    dve.wait_ge(s_x2t_ps, i - 1)
                dve.tensor_scalar(xn[:, i % 2, :], x_sb[:, i, :], sm[:, 4:5], sm[:, 7:8],
                                  ALU.subtract, ALU.mult).then_inc(s_x2, 1)

            for i in range(TILES + 3):
                if i < TILES:
                    attention_moments(i)
                if 1 <= i < TILES + 1:
                    first_residual(i - 1)
                if 2 <= i < TILES + 2:
                    second_norm(i - 2)
                if i >= 3:
                    dve.wait_ge(s_log_ps, i - 2)
                    dve.tensor_copy(logits[:, i - 3, :], ps[:, 4 + (i - 3) % 2, 0:E + 1]).then_inc(s_log, 1)
            dve.wait_ge(s_log, TILES)

            step(dve.tensor_reduce(rt[:, 0, :], logits[:, :, 0:E], AX.X, ALU.max))
            dve.tensor_scalar(rt[:, 0, :], rt[:, 0, :], -1.0, None, ALU.mult).then_inc(s_neg, 1)
            dve.memset(earlier[:, 0, :], 0.0).then_inc(s_own, 1)
            own[0] += 1
            dve.wait_ge(s_e1, TILES + 1)
            step(dve.reciprocal(rt[:, 2, :], rt[:, 1, :]))

            def per_tile(a):
                return a.rearrange("p (t o) -> p t o", o=1).broadcast_to([P, TILES, E])

            step(dve.tensor_tensor(out=prob_e, in0=prob_e, in1=per_tile(rt[:, 2, :]), op=ALU.mult))
            for i in range(TILES):
                dve.max(top[:, i, :], prob_e[:, i, :]).then_inc(s_own, 1)
            own[0] += TILES
            dve.wait_ge(s_own, own[0])
            for i in range(TILES):
                dve.match_replace(prob_r[:, i, :], top[:, i, :], prob_e[:, i, :], -1.0).then_inc(s_own, 1)
            own[0] += TILES
            dve.wait_ge(s_own, own[0])
            step(dve.tensor_scalar(chosen, prob_r, -1.0, None, ALU.is_equal))
            for i in range(TILES):
                ins = dve.tensor_tensor(out=earlier[:, i + 1, :], in0=earlier[:, i, :], in1=chosen[:, i, :], op=ALU.add)
                if i < TILES - 1:
                    step(ins)
            ins.then_inc(s_route, 1)
            step(dve.tensor_reduce(rt[:, 3, :], top[:, :, :], AX.X, ALU.add))
            step(dve.reciprocal(rt[:, 3, :], rt[:, 3, :]))
            step(dve.tensor_tensor(out=prob_e, in0=prob_e, in1=chosen, op=ALU.mult))
            dve.tensor_tensor(out=prob_e, in0=prob_e, in1=per_tile(rt[:, 3, :]), op=ALU.mult).then_inc(s_comb, 1)
            step(dve.tensor_scalar(rt[:, 4, :], rt[:, 4, :], 1.0, None, ALU.add))
            step(dve.reciprocal(rt[:, 4, :], rt[:, 4, :]))

            dve.wait_ge(s_cnt_ps, 1)
            dve.wait_ge(s_in[I_STEPS], 16)
            dve.wait_ge(s_in[I_ONES], 16)
            dve.wait_ge(s_in[I_COUNT], 16)
            dve.wait_ge(s_in[I_TOKEN], 16)
            step(dve.tensor_copy(n_col[:, 0:1], ps[0:E, 7, 0:1]))
            step(dve.tensor_scalar(n_cmp[:, :], steps_sb[:, :], n_col[:, 0:1], None, ALU.is_lt))
            step(dve.tensor_reduce(n_col[:, 1:2], n_cmp[:, :], AX.X, ALU.add))
            step(dve.tensor_scalar(n_col[:, 1:2], n_col[:, 1:2], 1.0, None, ALU.max))
            dve.tensor_scalar(n_rep, ones_sb[0:E, :], n_col[:, 1:2], None, ALU.mult).then_inc(s_cnt, 1)
            dve.wait_ge(s_ends_ps, 1)
            dve.tensor_copy(n_col[:, 2:3], ps[0:E, 7, 8:9]).then_inc(s_own, 1)
            dve.tensor_scalar(ends_i[:, :], ps[0:1, 7, 16:16 + E], 1.0, None, ALU.add).then_inc(s_tables, 1)
            own[0] += 1
            step(dve.tensor_copy(pairs_i[:, 0:1], ps[0:1, 7, 15 + E:16 + E]))
            dve.tensor_scalar(past_end, count_sb[0:E, :], n_col[:, 2:3], None, ALU.is_ge).then_inc(s_cnt, 1)
            dve.tensor_scalar(pairs_i[:, 1:2], pairs_i[:, 0:1], 1, None, ALU.logical_shift_right).then_inc(s_tables, 1)
            dve.wait_ge(s_slots_ps, 1)
            for half in range(2):
                dve.scalar_tensor_tensor(out=slots[:, 8 * half:8 * half + 8, :],
                                         in0=ps[:, half, :].rearrange("p (t e) -> p t e", e=E), scalar=1.0,
                                         in1=chosen[:, 8 * half:8 * half + 8, :], op0=ALU.add,
                                         op1=ALU.mult).then_inc(s_own, 1)
            own[0] += 2
            dve.wait_ge(s_own, own[0])
            for i in range(TILES):
                dve.max(slot_f[:, i, :], slots[:, i, :]).then_inc(s_own, 1)
            own[0] += TILES
            dve.wait_ge(s_own, own[0])
            step(dve.tensor_scalar(slot_i[:, :, :], slot_f[:, :, :], -1.0, None, ALU.add))
            dve.tensor_scalar(part_i[:, 0], slot_i[:, :, :], P - 1, None, ALU.bitwise_and).then_inc(s_own, 1)
            dve.tensor_scalar(part_i[:, 1], slot_i[:, :, :], 7, None, ALU.logical_shift_right).then_inc(s_own, 1)
            own[0] += 2
            dve.wait_ge(s_own, own[0])
            step(dve.tensor_copy(part_f[:, :, :, :], part_i[:, :, :, :]))
            dve.wait_ge(s_row_ps, 1)
            tile_expert = ps[0:1, 7, 96:96 + HIGH]
            step(dve.tensor_scalar(col_i[:, :], tile_expert, float(E - 1), None, ALU.min))
            dve.tensor_scalar(weights_i[:, :], tile_expert, float(E - 1), 1.0, ALU.min, ALU.add).then_inc(s_tables, 1)
            dve.tensor_scalar(ring_i[:, :], col_i[:, :], NW - 1, None, ALU.bitwise_and).then_inc(s_tables, 1)
            for m in range(TILES * K):
                t, k = divmod(m, K)
                if m >= RING:
                    dve.wait_ge(s_one_used, m - RING + 1)
                dve.tensor_scalar(low_1[:, m % RING, :], count_sb[:, 0:P], part_f[:, 0, t, k:k + 1], None, ALU.is_equal)
                dve.tensor_scalar(high_1[:, m % RING, :], count_sb[:, :], part_f[:, 1, t, k:k + 1], token_sb[:, t:t + 1],
                                  ALU.is_equal, ALU.mult).then_inc(s_high, 1)
            dve.wait_ge(s_one_used, TILES * K)
            step(dve.tensor_copy(table_f, ps[:, 6, 0:HIGH]))
            step(dve.tensor_scalar(table_z, table_f, 0.0, float(B * S + 1), ALU.is_equal, ALU.mult))
            step(dve.scalar_tensor_tensor(out=token_i[:, 0:HIGH], in0=table_f, scalar=-1.0, in1=table_z,
                                          op0=ALU.add, op1=ALU.add))
            dve.memset(token_i[:, HIGH:HIGH + 2], B * S).then_inc(s_table, 1)

            dve.wait_ge(s_table, 1)
            dve.wait_ge(s_tables, 4)
            wcol = small[:, 0, 0:2]
            pairs = dve.value_load(pairs_i[0:1, 1:2], min_val=HIGH // 2 - TILES * 2, max_val=HIGH // 2 - 1)

            def stage_gather(t, p):
                dve.tensor_scalar(idx[:, p, 0:1], token_i[:, bass.ts(t, 1)], B * S - 1, None, ALU.min).then_inc(s_idx, 1)

            def weight(t, p, r):
                dve.wait_ge(s_gather[p], r)
                col = dve.value_load(col_i[0:1, bass.ts(t, 1)], min_val=0, max_val=E - 1)
                dve.tensor_scalar(wcol[:, p:p + 1], rows[:, p, D:XROW][:, bass.ts(col, 1)], 1.0, None,
                                  ALU.mult).then_inc(s_weight, 1)

            def hide(t, p):
                dve.wait_ge(s_gate, t + 1)
                dve.wait_ge(s_weight, t + 1)
                dve.scalar_tensor_tensor(out=hidden[:, p, :], in0=gate[:, p, :], scalar=wcol[:, p:p + 1],
                                         in1=ps[:, 2 + p, F:GATEUP], op0=ALU.mult, op1=ALU.mult).then_inc(s_hid, 1)

            def take_y(t, p, r):
                dve.wait_ge(s_dn, t + 2)
                dve.wait_ge(s_scatter[p], r)
                dve.tensor_scalar(idx[:, p, 1:2], token_i[:, bass.ts(t, 1)], 0, None, ALU.add)
                dve.tensor_scalar(y_sb[:, p, :], ps[:, 5 + p, :], 1.0, None, ALU.mult).then_inc(s_y, 1)

            def take_hidden(t, p):
                dve.wait_ge(s_ht_ps, t + 1)
                dve.tensor_scalar(hidden_t[:, p, :], ps[:, 4, 0:P], 1.0, None, ALU.mult).then_inc(s_ht, 1)

            stage_gather(0, 0)
            stage_gather(1, 1)
            weight(0, 0, 16)
            stage_gather(2, 0)
            hide(0, 0)
            weight(1, 1, 16)
            stage_gather(3, 1)
            take_hidden(0, 0)
            with dve.Fori(0, pairs) as j:
                for p in range(2):
                    t = j * 2 + (p + 1)
                    hide(t, 1 - p)
                    dve.wait_ge(s_hid, t)
                    weight(t + 1, p, (j + 2) * 16)
                    take_y(t - 1, p, (j + 2) * 16)
                    stage_gather(t + 3, p)
                    take_hidden(t, 1 - p)
            take_y(pairs * 2, 0, (pairs + 2) * 16)

            def gather_sum(i):
                y = y_shared[:, i, :]
                b, t = divmod(i, TB)
                step(dve.scalar_tensor_tensor(out=y, in0=y, scalar=rt[:, 4, i:i + 1], in1=sums[:, b % 2, 0, t, :],
                                              op0=ALU.mult, op1=ALU.add))
                dve.tensor_tensor(out=y, in0=y, in1=sums[:, b % 2, 1, t, :], op=ALU.add).then_inc(s_sum, 1)

            def last_norm(b):
                dve.wait_ge(s_lnf, b + 1)
                step(dve.reciprocal(rstd[:, bass.ts(b, TB)], rstd[:, bass.ts(b, TB)]))
                for i in range(b * TB, (b + 1) * TB):
                    dve.tensor_scalar(y_shared[:, i, :], y_shared[:, i, :], moments[:, i, 0:1], rstd[:, i:i + 1],
                                      ALU.subtract, ALU.mult).then_inc(s_norm, 1)

            dve.wait_ge(s_sy, TILES)
            for b in range(B):
                dve.wait_ge(s_sums[b], 32)
                for i in range(b * TB, (b + 1) * TB):
                    gather_sum(i)
                dve.wait_ge(s_sum, (b + 1) * TB)
                for i in range(b * TB, (b + 1) * TB):
                    dve.bn_stats(stats[:, i, :], y_shared[:, i, :]).then_inc(s_own, 1)
                own[0] += TB
                dve.wait_ge(s_own, own[0])
                for i in range(b * TB, (b + 1) * TB):
                    dve.bn_aggr(moments[:, i, :], stats[:, i, :]).then_inc(s_own, 1)
                own[0] += TB
                dve.wait_ge(s_own, own[0])
                mv = moments[:, bass.ts(b, TB), 1]
                dve.tensor_scalar(mv, mv, EPS, None, ALU.add).then_inc(s_lnb, 1)
                if b >= 1:
                    last_norm(b - 1)
            last_norm(B - 1)


def _constants():
    idx = np.arange(0, DH, 2, dtype=np.float32)
    inv_freq = (np.float32(THETA) ** (-idx / np.float32(DH))).astype(np.float32)
    angles = np.arange(S, dtype=np.float32)[:, None] * inv_freq[None, :]
    cos, sin = np.cos(angles).astype(np.float32), np.sin(angles).astype(np.float32)
    rope = np.concatenate([np.repeat(cos, 2, axis=1), -sin, sin], axis=1)
    rope = np.ascontiguousarray(rope.reshape(TB, P, 2 * DH).transpose(1, 0, 2))
    mask = np.zeros((P, S), np.float32)
    mask[:, S - P:] = np.where(np.arange(P)[None, :] > np.arange(P)[:, None], MASKED, 0.0)
    headmask = (np.arange(P)[:, None] // DH == np.arange(HG)[None, :]).astype(np.float32)
    p = np.arange(P)
    e = np.arange(E)
    tables = {
        "rope": rope, "mask": mask, "headmask": headmask, "ident": np.eye(P),
        "before": p[:, None] < p[None, :],
        "ones": np.ones((P, P)),
        "upto": e[:, None] <= e[None, :],
        "below": P * (e[:, None] < e[None, :]),
        "steps": np.broadcast_to(P * np.arange(TILES), (E, TILES)),
        "count": np.broadcast_to(np.arange(HIGH), (P, HIGH)),
        "token": p[:, None] + P * np.arange(TILES)[None, :] + 1,
    }
    return {n: np.ascontiguousarray(t, dtype=np.float32) for n, t in tables.items()}


def kernel(L0_attn_x, L0_attn_Wq, L0_attn_Wk, L0_attn_Wv, L0_attn_Wo, L0_ffn_router_w, L0_ffn_Wg, L0_ffn_Wu,
           L0_ffn_Wd, L0_ffn_Wsg, L0_ffn_Wsu, L0_ffn_Wsd, L0_ffn_Wse):
    import concourse.bacc as bacc
    from concourse.bass_utils import run_bass_kernel_spmd

    def chunks(w):
        w = np.asarray(w)
        return w.T.reshape(-1, P, w.shape[0]).transpose(1, 0, 2)

    qkv = np.stack([chunks(w).reshape(P, DC, G, P) for w in (L0_attn_Wq, L0_attn_Wk, L0_attn_Wv)], axis=3)
    wg = np.concatenate([np.asarray(L0_ffn_Wg), np.asarray(L0_ffn_Wsg)[None]])
    wu = np.concatenate([np.asarray(L0_ffn_Wu), np.asarray(L0_ffn_Wsu)[None]])
    wd = np.concatenate([np.asarray(L0_ffn_Wd), np.asarray(L0_ffn_Wsd)[None]])
    up = np.concatenate([wg, wu], axis=1).transpose(0, 2, 1).reshape(E + 1, DC, P, GATEUP).transpose(0, 2, 1, 3)
    experts = np.concatenate([up.reshape(E + 1, P, DC * GATEUP), wd.transpose(0, 2, 1)], axis=2)
    arrays = {
        "x": np.asarray(L0_attn_x).reshape(B * S, D),
        "wqkv": qkv.reshape(P, DC, G, QKV),
        "wo": chunks(L0_attn_Wo),
        "router": chunks(np.concatenate([np.asarray(L0_ffn_router_w), np.asarray(L0_ffn_Wse)])),
        "experts": experts,
        **_constants(),
    }
    arrays = {n: np.ascontiguousarray(a) for n, a in arrays.items()}
    nc = bacc.Bacc("TRN2", target_bir_lowering=False, num_devices=1)
    args = [nc.dram_tensor(n, a.shape, mybir.dt.from_np(a.dtype), kind="ExternalInput").ap() for n, a in arrays.items()]
    out = nc.dram_tensor("out", (B * S, D), FP32, kind="ExternalOutput").ap()
    sandwich_kernel(nc, *args, out)
    r = run_bass_kernel_spmd(nc, [arrays], core_ids=[0])
    return r.results[0]["out"].reshape(B, S, D)
```

```python
from contextlib import ExitStack

import numpy as np

import concourse.bass as bass
from concourse import mybir

FP32 = mybir.dt.float32
FP16 = mybir.dt.float16
INT32 = mybir.dt.int32
ACT = mybir.ActivationFunctionType
ALU = mybir.AluOpType
AX = mybir.AxisListType

P = 128
B, S, D = 4, 512, 512
H, DH = 16, 32
E, K, F = 64, 8, 128
THETA = 10000.0
EPS = 1e-5
TB = S // P
TILES = B * TB
DC = D // P
HG = P // DH
G = H // HG
QKV = 3 * P
UNITS = H * TB
GU = UNITS // G
GATEUP = 2 * F
MASKED = -1.0e38
SCALE = float(DH) ** -0.5
WCOLS = DC * GATEUP + D
NW = 8
XROW = D + E
HIGH = (B * S * K + E * (P - 1)) // P + 1
RING = 8


STEPS = {"proj": (1, 3, 6, 10), "qkt": (4, 6, 9, 13)}
LAST_STEPS = {"xt": (0, 2, 4, 6), "proj": (2, 5, 8, 11), "qkt": (7, 9, 12, 15)}
FIRST_STEPS = [("xt", 0), ("xt", 1), ("proj", 0), ("xt", 2), ("proj", 1), ("xt", 3), ("proj", 2), ("qkt", 0),
               ("proj", 3), ("qkt", 1), ("qkt", 2), ("qkt", 3)]
LAST_ON_DVE = (TILES - 3, TILES - 1)
LAST_ON_POOL = tuple(i for i in range(TILES) if i not in LAST_ON_DVE)
NORM_X_AT = (2 * GU + 13, 2 * GU + 15, 3 * GU + 1, 3 * GU + 3)


def misc_steps(g, s, last):
    if g == G - 1 and last:
        return []
    steps = STEPS if g < G - 1 else LAST_STEPS
    return [(kind, t) for t in range(TB) for kind in steps if steps[kind][t] == s]


def sandwich_kernel(nc, x, wqkv, wo, router, experts, rope, mask, headmask, ident, before, ones, upto, below,
                    steps, count, token, out):
    ctx = ExitStack()
    with ctx:
        def sb(name, shape, dtype=FP32):
            return ctx.enter_context(nc.sbuf_tensor(name, shape, dtype))

        def sem(name):
            return ctx.enter_context(nc.semaphore(name))

        x_sb = sb("x_sb", [P, TILES, D])
        attn_t = sb("attn_t", [P, TILES, G, P])
        x2_t = sb("x2_t", [P, DC, B * S])
        wo_sb = sb("wo_sb", [P, G, D])
        router_sb = sb("router_sb", [P, DC, E + 1])
        rope_sb = sb("rope_sb", [P, TB, 2 * DH])
        mask_sb = sb("mask_sb", [P, S])
        hmask_sb = sb("hmask_sb", [P, HG])
        ident_sb = sb("ident_sb", [P, P])
        before_sb = sb("before_sb", [P, P])
        ones_sb = sb("ones_sb", [P, P])
        upto_sb = sb("upto_sb", [E, E])
        below_sb = sb("below_sb", [E, E])
        steps_sb = sb("steps_sb", [E, TB * B])
        count_sb = sb("count_sb", [P, HIGH])
        count_h = sb("count_h", [P, HIGH], FP16)
        token_sb = sb("token_sb", [P, TILES])
        logits = sb("logits", [P, TILES, E + 1])
        stats = sb("stats", [P, TILES, 6])
        moments = sb("moments", [P, TILES, 2])
        rstd = sb("rstd", [P, TILES])
        small = sb("small", [P, 4, 8])
        top = sb("top", [P, TILES, K])
        rt = sb("rt", [P, 5, TILES])
        slot_i = sb("slot_i", [P, TILES, K], INT32)
        part_i = sb("part_i", [P, 2, TILES, K], INT32)
        low_1 = sb("low_1", [P, RING, P], FP16)
        high_1 = sb("high_1", [P, RING, HIGH], FP16)
        n_col = sb("n_col", [E, 4])
        n_cmp = sb("n_cmp", [E, TILES])
        ends_i = sb("ends_i", [1, E], INT32)
        pairs_i = sb("pairs_i", [1, 2], INT32)
        weights_i = sb("weights_i", [1, HIGH], INT32)
        ring_i = sb("ring_i", [1, HIGH // 2, 4], INT32)
        col_i = sb("col_i", [1, HIGH], INT32)
        token_i = sb("token_i", [P, HIGH + 2], INT32)
        idx = sb("idx", [P, 2, 2], INT32)

        big = sb("big", [P, NW * WCOLS])
        wqkv_sb = big[:, 0:DC * G * QKV].rearrange("p (c g n) -> p c g n", c=DC, g=G)
        x_t = big[:, 6144:8192].rearrange("p (c n) -> p c n", c=DC)
        q_pad = big[:, 8192:12288].rearrange("p (a h n) -> p a h n", a=2, h=HG)
        w_ring = big[:, :].rearrange("p (r n) -> p r n", r=NW)

        work = sb("work", [P, 5120])
        probs = work[:, 0:2048].rearrange("p (a n) -> p a n", a=4)
        k_t = work[:, 2048:3072].rearrange("p (a n) -> p a n", a=2)
        roped = work[:, 3072:3584].rearrange("p (a n) -> p a n", a=2)
        rope_cos = work[:, 3584:3840]
        rope_sin = work[:, 3840:4096]
        xn = work[:, 4096:5120].rearrange("p (a n) -> p a n", a=2)
        delta = work[:, 2048:3072].rearrange("p (a n) -> p a n", a=2)
        rows = work[:, 0:2 * XROW].rearrange("p (a n) -> p a n", a=2)
        rows_t = work[:, 1152:2176].rearrange("p (a c n) -> p a c n", a=2, c=DC)
        y_sb = work[:, 2176:3200].rearrange("p (a n) -> p a n", a=2)
        gate = work[:, 3200:3456].rearrange("p (a n) -> p a n", a=2)
        hidden = work[:, 3456:3712].rearrange("p (a n) -> p a n", a=2)
        hidden_t = work[:, 3712:3968].rearrange("p (a n) -> p a n", a=2)
        up_s = work[:, 2176:2432].rearrange("p (a n) -> p a n", a=2)

        qkv_all = sb("qkv_all", [P, 2 * TB * QKV])
        qkv = qkv_all[:, :].rearrange("p (a t n) -> p a t n", a=2, t=TB)
        chosen = qkv_all[:, 0:1024].rearrange("p (t e) -> p t e", e=E)
        earlier = qkv_all[:, 1024:2048 + E].rearrange("p (t e) -> p t e", e=E)
        table_f = qkv_all[:, 2112:2112 + HIGH]
        table_z = qkv_all[:, 2112 + HIGH:2112 + 2 * HIGH]
        slot_f = work[:, 0:P].rearrange("p (t k) -> p t k", k=K)
        part_f = work[:, P:3 * P].rearrange("p (a t k) -> p a t k", a=2, k=K)
        n_rep = qkv_all[0:E, 2496:2496 + P]
        past_end = qkv_all[0:E, 2624:2624 + HIGH]

        prob_e = wo_sb[:, 0:2, :].rearrange("p a n -> p (a n)").rearrange("p (t e) -> p t e", e=E)
        prob_r = wo_sb[:, 2:4, :].rearrange("p a n -> p (a n)").rearrange("p (t e) -> p t e", e=E)
        slots = prob_r
        probs_t = x2_t[:, 0:2, :].rearrange("p c n -> p (c n)").rearrange("p (a k n) -> p a k n", a=8, k=TB)
        zeros = x2_t[:, 2:4, :]
        sums = x2_t[:, :, :].rearrange("p c n -> p (c n)").rearrange("p (a s t n) -> p a s t n", a=2, s=2, t=TB)
        y_shared = attn_t[:, :, :, :].rearrange("p t g n -> p t (g n)")

        neg_max = sb("neg_max", [P, 4])
        den = sb("den", [P, 4])
        rden = sb("rden", [P, 4])

        x2_rows = nc.dram_tensor("x2_rows", (B * S, XROW), FP32).ap()
        sum_rows = [nc.dram_tensor(f"sum_rows{p}", (B * S, D), FP32).ap() for p in range(2)]

        ps = ctx.enter_context(nc.psum_tensor("ps", [P, 8, 512], FP32))
        s_bank = [ps[:, i, :] for i in range(3)]
        pt_bank = [ps[:, 4 + i, :] for i in range(2)]
        av_bank = ps[:, 6, :]
        turn_bank = ps[:, 3, :]
        qkv_bank = ps[:, 7, :]

        NIN = 15
        s_in = [sem(f"s_in{i}") for i in range(NIN)]
        s_xin = [sem(f"s_xin{i}") for i in range(B)]
        s_moments = sem("s_moments")
        s_ln = sem("s_ln")
        s_std = sem("s_std")
        s_xn = sem("s_xn")
        s_xt_ps = sem("s_xt_ps")
        s_xt = sem("s_xt")
        s_qkv_ps = sem("s_qkv_ps")
        s_qkv = sem("s_qkv")
        s_rtmp = sem("s_rtmp")
        s_rope = sem("s_rope")
        s_qkt_ps = sem("s_qkt_ps")
        s_qkt = sem("s_qkt")
        s_scored = sem("s_scored")
        s_masked = sem("s_masked")
        s_exp = sem("s_exp")
        s_recip = sem("s_recip")
        s_seen = sem("s_seen")
        s_probs = sem("s_probs")
        s_turned = sem("s_turned")
        s_pt = sem("s_pt")
        s_av = sem("s_av")
        s_attn = sem("s_attn")
        s_own = sem("s_own")
        s_y_ps = sem("s_y_ps")
        s_var = sem("s_var")
        s_sq = sem("s_sq")
        s_stat = sem("s_stat")
        s_x1 = sem("s_x1")
        s_x2 = sem("s_x2")
        s_x2t_ps = sem("s_x2t_ps")
        s_x2t = sem("s_x2t")
        s_log_ps = sem("s_log_ps")
        s_log = sem("s_log")
        s_zero = sem("s_zero")
        s_neg = sem("s_neg")
        s_e1 = sem("s_e1")
        s_sigmoid = sem("s_sigmoid")
        s_route = sem("s_route")
        s_comb = sem("s_comb")
        s_cnt_ps = sem("s_cnt_ps")
        s_cnt = sem("s_cnt")
        s_ends_ps = sem("s_ends_ps")
        s_slots_ps = sem("s_slots_ps")
        s_row_ps = sem("s_row_ps")
        s_tables = sem("s_tables")
        s_high = sem("s_high")
        s_one_used = sem("s_one_used")
        s_table = sem("s_table")
        s_sgu = sem("s_sgu")
        s_silu = sem("s_silu")
        s_up = sem("s_up")
        s_shid = sem("s_shid")
        s_sht = sem("s_sht")
        s_shte = sem("s_shte")
        s_sdn = sem("s_sdn")
        s_sy = sem("s_sy")
        s_ready = sem("s_ready")
        s_idx = sem("s_idx")
        s_weight = sem("s_weight")
        s_issue = sem("s_issue")
        s_xg_ps = sem("s_xg_ps")
        s_xg = sem("s_xg")
        s_gu = sem("s_gu")
        s_gate = sem("s_gate")
        s_hid = sem("s_hid")
        s_ht_ps = sem("s_ht_ps")
        s_ht = sem("s_ht")
        s_dn = sem("s_dn")
        s_y = sem("s_y")
        s_sum = sem("s_sum")
        s_lnb = sem("s_lnb")
        s_lnf = sem("s_lnf")
        s_lnd = sem("s_lnd")
        s_norm = sem("s_norm")
        s_fin = sem("s_fin")
        s_fin_dve = sem("s_fin_dve")
        s_out = sem("s_out")
        s_x2d = [sem(f"s_x2d{p}") for p in range(2)]
        s_combd = sem("s_combd")
        s_wl = [sem(f"s_wl{r}") for r in range(NW)]
        s_ws = sem("s_ws")
        s_gather = [sem(f"s_gather{p}") for p in range(2)]
        s_scatter = [sem(f"s_scatter{p}") for p in range(2)]
        s_sums = [sem(f"s_sums{p}") for p in range(4)]

        block = ctx.enter_context(nc.Block())
        x_v = x.rearrange("(t p) d -> p t d", p=P)
        out_v = out.rearrange("(t p) d -> p t d", p=P)

        sums_v = [r.rearrange("(t p) d -> p t d", p=P) for r in sum_rows]
        x2_v = x2_rows.rearrange("(t p) d -> p t d", p=P)
        LOADS = [(ident_sb[:, :], ident), (rope_sb[:, :, :], rope), (hmask_sb[:, :], headmask),
                 (mask_sb[:, :], mask), (wo_sb[:, :, :], wo), (router_sb[:, :, :], router),
                 (before_sb[:, :], before), (ones_sb[:, :], ones), (upto_sb[:, :], upto), (below_sb[:, :], below),
                 (steps_sb[:, :], steps), (count_sb[:, :], count), (token_sb[:, :], token)]
        I_IDENT, I_ROPE, I_HMASK, I_MASK, I_WO, I_ROUTER, I_BEFORE, I_ONES, I_UPTO, I_BELOW, I_STEPS, I_COUNT, I_TOKEN, I_WQKV,\
            I_WQKV0 = range(NIN)

        def every_batch(eng, body):
            with eng.Fori(0, B - 1) as b:
                body(b, False)
            body(B - 1, True)

        def attention_roots(i):
            return i + 1 + max(i - 2, 0)

        def residual_roots(i):
            return min(i + 3, TILES) + i + 1

        @block.sync
        def _(sp):
            sp.dma_start(x_sb[:, 0:TB, :], x_v[:, 0:TB, :]).then_inc(s_xin[0], 16)
            sp.dma_start(ident_sb[:, :], ident).then_inc(s_in[I_IDENT], 16)
            sp.dma_start(wqkv_sb[:, :, 0, :], wqkv[:, :, 0, :]).then_inc(s_in[I_WQKV0], 16)
            for i in (I_ROPE, I_HMASK, I_MASK):
                sp.dma_start(*LOADS[i]).then_inc(s_in[i], 16)
            sp.dma_start(wqkv_sb[:, :, 1:G, :], wqkv[:, :, 1:G, :]).then_inc(s_in[I_WQKV], 16)
            for b in range(1, B):
                sp.dma_start(x_sb[:, b * TB:(b + 1) * TB, :], x_v[:, b * TB:(b + 1) * TB, :]).then_inc(s_xin[b], 16)
            for i in range(I_WO, len(LOADS)):
                sp.dma_start(*LOADS[i]).then_inc(s_in[i], 16)
            sp.wait_ge(s_attn, B * G * TB)
            for r in range(NW - 1):
                sp.dma_start(w_ring[:, r, :], experts[r]).then_inc(s_wl[r], 16)
            sp.dma_start(w_ring[:, NW - 1, :], experts[E]).then_inc(s_ws, 16)
            for i in range(TILES):
                sp.wait_ge(s_x2, i + 1)
                sp.dma_start(x2_v[:, i, 0:D], xn[:, i % 2, :]).then_inc(s_x2d[i % 2], 16)
            sp.wait_ge(s_comb, 1)
            with nc.allow_non_contiguous_dma(reason="64 weights beside each row"):
                sp.dma_start(x2_v[:, :, D:XROW], prob_e).then_inc(s_combd, 16)
            sp.wait_ge(s_sdn, TILES)
            sp.dma_start(w_ring[:, NW - 1, :], experts[NW - 1]).then_inc(s_wl[NW - 1], 16)
            for r in range(NW):
                sp.wait_ge(s_wl[r], 16)
                sp.sem_inc(s_ready, 1)
            sp.wait_ge(s_tables, 4)
            with sp.Fori(0, E // NW - 1) as j:
                for r in range(NW):
                    end = sp.value_load(ends_i[0:1, bass.ts(j * NW + r, 1)], min_val=1, max_val=HIGH)
                    sp.wait_ge(s_dn, end)
                    sp.dma_start(w_ring[:, r, :], experts[j * NW + (r + NW)]).then_inc(s_wl[r], 16)
                    if r >= 2:
                        sp.wait_ge(s_wl[r - 2], (j + 2) * 16)
                        sp.sem_inc(s_ready, 1)
                for r in range(NW - 2, NW):
                    sp.wait_ge(s_wl[r], (j + 2) * 16)
                    sp.sem_inc(s_ready, 1)
            pairs = sp.value_load(pairs_i[0:1, 1:2], min_val=HIGH // 2 - TILES * 2, max_val=HIGH // 2 - 1)
            for p in range(2):
                sp.wait_ge(s_scatter[p], (pairs + (3 - p)) * 16)
            for b in range(B):
                if b >= 2:
                    sp.wait_ge(s_sum, (b - 1) * TB)
                for p in range(2):
                    sp.dma_start(sums[:, b % 2, p, :, :], sums_v[p][:, b * TB:(b + 1) * TB, :]).then_inc(s_sums[b], 16)
            for i in range(TILES):
                if i in LAST_ON_POOL:
                    sp.wait_ge(s_fin, LAST_ON_POOL.index(i) + 1)
                else:
                    sp.wait_ge(s_fin_dve, LAST_ON_DVE.index(i) + 1)
                sp.dma_start(out_v[:, i, :], x_sb[:, i, :]).then_inc(s_out, 16)
            sp.wait_ge(s_out, 16 * TILES)

        @block.gpsimd
        def _(pool):
            def rope_group_tile(i4, g, t):
                n = (i4 + g) * TB + t
                src = qkv[:, g % 2, t, 0:2 * P]
                pair = src.rearrange("p (h j e) -> p h j e", h=2 * HG, e=2)
                sin_pair = rope_sin[:, :].rearrange("p (h j e) -> p h j e", h=2 * HG, e=2)
                heads = src.rearrange("p (h d) -> p h d", h=2 * HG)
                cos = rope_sb[:, t, 0:DH].rearrange("p (o d) -> p o d", o=1).broadcast_to([P, 2 * HG, DH])
                nsin = rope_sb[:, t, DH:DH + 16].rearrange("p (o d) -> p o d", o=1).broadcast_to([P, 2 * HG, 16])
                psin = rope_sb[:, t, DH + 16:DH + 32].rearrange("p (o d) -> p o d", o=1).broadcast_to([P, 2 * HG, 16])
                pool.wait_ge(s_qkv, n + 1)
                pool.tensor_tensor(out=rope_cos[:, :].rearrange("p (h d) -> p h d", h=2 * HG), in0=heads,
                                   in1=cos, op=ALU.mult).then_inc(s_rtmp, 1)
                pool.tensor_tensor(out=sin_pair[:, :, :, 0], in0=pair[:, :, :, 1], in1=nsin,
                                   op=ALU.mult).then_inc(s_rtmp, 1)
                pool.tensor_tensor(out=sin_pair[:, :, :, 1], in0=pair[:, :, :, 0], in1=psin,
                                   op=ALU.mult).then_inc(s_rtmp, 1)
                pool.wait_ge(s_rtmp, (n + 1) * 3)
                pool.tensor_tensor(out=roped[:, t % 2, :], in0=rope_cos[:, :], in1=rope_sin[:, :],
                                   op=ALU.add).then_inc(s_rope, 1)
                pool.wait_ge(s_rope, n + 1)

            pool.memset(zeros, 0.0).then_inc(s_zero, 1)
            pool.wait_ge(s_in[I_ROPE], 16)
            for t in range(TB):
                if t >= 2:
                    pool.wait_ge(s_qkt_ps, t - 1)
                rope_group_tile(0, 0, t)
            pool.wait_ge(s_zero, 1)
            for b in range(1, B):
                pool.wait_ge(s_xin[b], 16)
            for p in range(2):
                for half in range(2):
                    pool.dma_start(sums_v[p][:, 8 * half:8 * half + 8, :],
                                   zeros.rearrange("p c n -> p (c n)").rearrange("p (t n) -> p t n", n=D)).then_inc(s_scatter[p], 16)

            def batch(b, last):
                for g in range(1, G + (not last)):
                    for t in range(TB):
                        rope_group_tile(b * G, g, t)

            every_batch(pool, batch)

            for i in range(TILES):
                pool.wait_ge(s_stat, i + 1)
                pool.tensor_tensor(out=x_sb[:, i, :], in0=x_sb[:, i, :], in1=delta[:, i % 2, :],
                                   op=ALU.add).then_inc(s_x1, 1)
            for i in range(TILES):
                pool.wait_ge(s_up, i + 1)
                if i >= 2:
                    pool.wait_ge(s_sht, i - 1)
                pool.tensor_tensor(out=hidden[:, i % 2, :], in0=gate[:, i % 2, :], in1=up_s[:, i % 2, :],
                                   op=ALU.mult).then_inc(s_shid, 1)

            def gather(p):
                pool.indirect_dma_start(rows[:, p, :], None, x2_rows,
                                        bass.IndirectOffsetOnAxis(ap=idx[:, p, 0:1], axis=0)).then_inc(s_gather[p], 16)

            def scatter(p):
                pool.indirect_dma_start(sum_rows[p], bass.IndirectOffsetOnAxis(ap=idx[:, p, 1:2], axis=0), y_sb[:, p, :],
                                        None, bounds_check=last_row, oob_is_err=False,
                                        compute_op=ALU.add).then_inc(s_scatter[p], 16)

            last_row = pool.to_reg(B * S - 1)
            for p in range(2):
                pool.wait_ge(s_x2d[p], 16 * (TILES // 2))
            pool.wait_ge(s_combd, 16)
            pool.wait_ge(s_sht, TILES)
            pool.wait_ge(s_shte, TILES)
            pool.wait_ge(s_tables, 4)
            pairs = pool.value_load(pairs_i[0:1, 1:2], min_val=HIGH // 2 - TILES * 2, max_val=HIGH // 2 - 1)
            for t in range(4):
                pool.wait_ge(s_idx, t + 1)
                if t >= 2:
                    pool.wait_ge(s_xg_ps, t - 1)
                    pool.wait_ge(s_weight, t - 1)
                gather(t % 2)
            with pool.Fori(0, pairs) as j:
                for p in range(2):
                    t = j * 2 + (p + 2)
                    pool.wait_ge(s_idx, t + 3)
                    pool.wait_ge(s_xg_ps, t + 1)
                    pool.wait_ge(s_weight, t + 1)
                    pool.sem_inc(s_issue, 1)
                    gather(p)
                    pool.wait_ge(s_y, t - 1)
                    pool.sem_inc(s_issue, 1)
                    scatter(p)
            pool.wait_ge(s_y, pairs * 2 + 1)
            pool.sem_inc(s_issue, 1)
            scatter(0)
            for p in range(2):
                pool.wait_ge(s_gather[p], (pairs + 2) * 16)
            for i in LAST_ON_POOL:
                pool.wait_ge(s_norm, i + 1)
                pool.tensor_tensor(out=x_sb[:, i, :], in0=x_sb[:, i, :], in1=y_shared[:, i, :],
                                   op=ALU.add).then_inc(s_fin, 1)

        @block.scalar
        def _(act):
            def root(first, last, k):
                act.wait_ge(s_ln, k)
                act.activation(rstd[:, first * TB:last * TB], moments[:, first * TB:last * TB, 1],
                               ACT.Sqrt).then_inc(s_std, 1)

            root(0, 1, 1)

            def evac_xt(b4, t):
                act.wait_ge(s_xt_ps, b4 + t + 1)
                act.activation(x_t[:, :, bass.ts(t, P)], turn_bank.rearrange("p (c n) -> p c n", c=DC),
                               ACT.Copy).then_inc(s_xt, 1)

            def evac_qkv(i4, g, t):
                n = (i4 + g) * TB + t
                act.wait_ge(s_qkv_ps, n + 1)
                act.activation(qkv[:, g % 2, t, :], qkv_bank[:, 0:QKV], ACT.Copy).then_inc(s_qkv, 1)

            for kind, t in FIRST_STEPS:
                if kind == "xt":
                    evac_xt(0, t)
                if kind == "proj":
                    evac_qkv(0, 0, t)
            root(1, B, 3)

            def exp(b, u):
                act.wait_ge(s_masked, b * UNITS + (u + 1))
                n = (u % GU // HG + 1) * P
                act.activation(probs[:, u % 4, 0:n], s_bank[u % 3][:, 0:n], ACT.Exp, bias=neg_max[:, u % 4:u % 4 + 1],
                               scale=-1.0, accum_out=den[:, u % 4:u % 4 + 1]).then_inc(s_exp, 1)

            def evac_pt(b, u):
                qt = u % GU // HG
                act.wait_ge(s_turned, b * UNITS + (u + 1))
                act.activation(probs_t[:, u % 8, 0:qt + 1, :],
                               pt_bank[u % 2].rearrange("p (k n) -> p k n", k=TB)[:, 0:qt + 1, :],
                               ACT.Copy).then_inc(s_pt, 1)

            def evac_attn(b, n):
                g, qt = divmod(n, TB)
                act.wait_ge(s_av, b * (G * TB) + (n + 1))
                act.activation(attn_t[:, b * TB + qt, g, :], av_bank[:, 0:P], ACT.Copy).then_inc(s_attn, 1)

            def batch(b, last):
                for u in range(3):
                    exp(b, u)
                for u in range(UNITS):
                    g, s = divmod(u, GU)
                    evac_pt(b, u)
                    if u + 3 < UNITS:
                        exp(b, u + 3)
                    if u % HG == 0 and u > 0:
                        evac_attn(b, u // HG - 1)
                    for kind, t in misc_steps(g, s, last):
                        if kind == "xt":
                            evac_xt((b + 1) * TB, t)
                        if kind == "proj":
                            evac_qkv(b * G, g + 1, t)
                evac_attn(b, G * TB - 1)

            every_batch(act, batch)

            for i in range(TILES + 5):
                if i < TILES:
                    act.wait_ge(s_var, attention_roots(i))
                    act.activation(small[:, i % 4, 2:3], small[:, i % 4, 1:2], ACT.Sqrt).then_inc(s_sq, 1)
                if 2 <= i < TILES + 2:
                    k = i - 2
                    act.wait_ge(s_var, residual_roots(k))
                    act.activation(small[:, k % 4, 6:7], small[:, k % 4, 5:6], ACT.Sqrt).then_inc(s_sq, 1)
                if i == 4:
                    for p in range(2):
                        act.wait_ge(s_scatter[p], 32)
                if 4 <= i < TILES + 4:
                    k = i - 4
                    act.wait_ge(s_x2t_ps, k + 1)
                    act.activation(x2_t[:, :, bass.ts(k, P)], ps[:, 2 + k % 2, :].rearrange("p (c n) -> p c n", c=DC),
                                   ACT.Copy).then_inc(s_x2t, 1)
                if i >= 5:
                    k = i - 5
                    act.wait_ge(s_log_ps, k + 1)
                    act.activation(logits[:, k, :], ps[:, 4 + k % 2, 0:E + 1], ACT.Copy).then_inc(s_log, 1)
            act.wait_ge(s_neg, 1)
            for i in range(TILES):
                act.activation(prob_e[:, i, :], logits[:, i, 0:E], ACT.Exp, bias=rt[:, 0, i:i + 1],
                               accum_out=rt[:, 1, i:i + 1]).then_inc(s_e1, 1)
            act.activation(rt[:, 4, :], logits[:, :, E], ACT.Exp, scale=-1.0).then_inc(s_e1, 1)

            for i in range(TILES + 1):
                if i < TILES:
                    act.wait_ge(s_sgu, i + 1)
                    if i >= 2:
                        act.wait_ge(s_shid, i - 1)
                    act.activation(gate[:, i % 2, :], ps[:, 2 + i % 2, 0:F], ACT.Silu).then_inc(s_silu, 1)
                    act.activation(up_s[:, i % 2, :], ps[:, 2 + i % 2, F:GATEUP], ACT.Copy).then_inc(s_up, 1)
                if i >= 1:
                    k = i - 1
                    act.wait_ge(s_sht, k + 1)
                    act.activation(hidden_t[:, k % 2, :], ps[:, 4, 0:P], ACT.Copy).then_inc(s_shte, 1)
                    act.wait_ge(s_sdn, k + 1)
                    if k == 0:
                        act.wait_ge(s_sigmoid, 1)
                    act.activation(y_shared[:, k, :], ps[:, 5, :], ACT.Copy, scale=rt[:, 4, k:k + 1]).then_inc(s_sy, 1)

            act.wait_ge(s_tables, 4)
            pairs = act.value_load(pairs_i[0:1, 1:2], min_val=HIGH // 2 - TILES * 2, max_val=HIGH // 2 - 1)

            def turned(t, p):
                need = act.value_load(weights_i[0:1, bass.ts(t, 1)], min_val=1, max_val=E)
                act.wait_ge(s_ready, need)
                act.wait_ge(s_xg_ps, t + 1)
                act.activation(rows_t[:, p, :, :], ps[:, p, :].rearrange("p (c n) -> p c n", c=DC),
                               ACT.Copy).then_inc(s_xg, 1)

            def silu(t, p):
                act.wait_ge(s_gu, t + 1)
                act.activation(gate[:, p, :], ps[:, 2 + p, 0:F], ACT.Silu).then_inc(s_gate, 1)

            turned(0, 0)
            silu(0, 0)
            turned(1, 1)
            with act.Fori(0, pairs) as j:
                for p in range(2):
                    t = j * 2 + (p + 1)
                    silu(t, (p + 1) % 2)
                    turned(t + 1, p)
            act.preload_act_table(ACT.Sqrt)
            for b in range(B):
                act.wait_ge(s_lnb, b + 1)
                act.activation(rstd[:, bass.ts(b, TB)], moments[:, bass.ts(b, TB), 1], ACT.Sqrt).then_inc(s_lnf, 1)
                act.wait_ge(s_lnd, b + 1)
                for i in range(b * TB, (b + 1) * TB):
                    act.activation(y_shared[:, i, :], y_shared[:, i, :], ACT.Identity, bias=moments[:, i, 0:1],
                                   scale=rstd[:, i:i + 1]).then_inc(s_norm, 1)

        @block.tensor
        def _(pe):
            def xt(b4, t):
                pe.wait_ge(s_xn, b4 + t + 1)
                if t == 0 and not isinstance(b4, int):
                    pe.wait_ge(s_qkt, b4 * G)
                elif t > 0:
                    pe.wait_ge(s_xt, b4 + t)
                for c in range(DC):
                    mm = pe.transpose(turn_bank[:, bass.ts(c, P)], xn[:, t % 2, bass.ts(c, P)], ident_sb[:, :])
                mm.then_inc(s_xt_ps, 1)

            def proj(i4, g, t, after_xt=None):
                if after_xt is not None:
                    pe.wait_ge(s_xt, after_xt + t + 1)
                n = (i4 + g) * TB + t
                if not (isinstance(n, int) and n == 0):
                    pe.wait_ge(s_qkv, n)
                for c in range(DC):
                    mm = pe.matmul(qkv_bank[:, 0:QKV], x_t[:, c, bass.ts(t, P)], wqkv_sb[:, c, g % G, :],
                                   start=(c == 0), stop=(c == DC - 1))
                mm.then_inc(s_qkv_ps, 1)

            def qkt(i4, g, t, after_xt=None):
                n = (i4 + g) * TB + t
                pe.wait_ge(s_rope, n + 1)
                if after_xt is not None:
                    pe.wait_ge(s_xt, after_xt)
                elif not (isinstance(n, int) and n == 0):
                    pe.wait_ge(s_qkt, n)
                for c in range(2):
                    mm = pe.transpose(turn_bank[:, bass.ts(c, P)], roped[:, t % 2, bass.ts(c, P)], ident_sb[:, :])
                mm.then_inc(s_qkt_ps, 1)

            pe.wait_ge(s_in[I_IDENT], 16)
            for kind, t in FIRST_STEPS:
                if kind == "xt":
                    xt(0, t)
                if kind == "proj":
                    if t == 0:
                        pe.wait_ge(s_in[I_WQKV0], 16)
                    proj(0, 0, t, after_xt=0)
                if kind == "qkt":
                    qkt(0, 0, t, after_xt=TB if t == 0 else None)
            pe.wait_ge(s_in[I_WQKV], 16)

            def score(b, u):
                g, (qt, h) = u // GU, divmod(u % GU, HG)
                pe.wait_ge(s_qkt, (b * G + g) * TB + (qt + 1))
                n = (qt + 1) * P
                pe.matmul(s_bank[u % 3][:, 0:n], q_pad[:, g % 2, h, bass.ts(qt, P)], k_t[:, g % 2, 0:n],
                          start=True, stop=True).then_inc(s_scored, 1)

            def turn(b, u):
                qt = u % GU // HG
                pe.wait_ge(s_probs, b * UNITS + (u + 1))
                if u >= 2:
                    pe.wait_ge(s_pt, b * UNITS + (u - 1))
                for k in range(qt + 1):
                    mm = pe.transpose(pt_bank[u % 2][:, bass.ts(k, P)], probs[:, u % 4, bass.ts(k, P)], ident_sb[:, :])
                mm.then_inc(s_turned, 1)

            def weigh(b, n):
                g, qt = divmod(n, TB)
                if n >= 1:
                    pe.wait_ge(s_attn, b * (G * TB) + n)
                pe.wait_ge(s_pt, b * UNITS + HG * (n + 1))
                for k in range(qt + 1):
                    for h in range(HG):
                        v0 = 2 * P + DH * h
                        mm = pe.matmul(av_bank[DH * h:DH * (h + 1), 0:P], qkv[:, g % 2, k, v0:v0 + DH],
                                       probs_t[:, HG * (n % 2) + h, k, :], start=(k == 0), stop=(k == qt))
                mm.then_inc(s_av, 1)

            def batch(b, last):
                for u in range(3):
                    score(b, u)
                for u in range(UNITS):
                    g, s = divmod(u, GU)
                    turn(b, u)
                    if u + 3 < UNITS:
                        score(b, u + 3)
                    if u % HG == 0 and u > 0:
                        weigh(b, u // HG - 1)
                    for kind, t in misc_steps(g, s, last):
                        if kind == "xt":
                            xt((b + 1) * TB, t)
                        if kind == "proj":
                            proj(b * G, g + 1, t, after_xt=(b + 1) * TB if g == G - 1 else None)
                        if kind == "qkt":
                            qkt(b * G, g + 1, t, after_xt=(b + 2) * TB if g == G - 1 and t == 0 else None)
                weigh(b, G * TB - 1)

            every_batch(pe, batch)

            pe.wait_ge(s_attn, B * G * TB)
            pe.wait_ge(s_in[I_WO], 16)
            pe.wait_ge(s_in[I_ROUTER], 16)

            def project(i):
                if i >= 2:
                    pe.wait_ge(s_stat, i - 1)
                for g in range(G):
                    mm = pe.matmul(ps[:, i % 2, :], attn_t[:, i, g, :], wo_sb[:, g, :], start=(g == 0), stop=(g == G - 1))
                mm.then_inc(s_y_ps, 1)

            def turn_x2(i):
                pe.wait_ge(s_x2, i + 1)
                if i >= 2:
                    pe.wait_ge(s_x2t, i - 1)
                for c in range(DC):
                    mm = pe.transpose(ps[:, 2 + i % 2, bass.ts(c, P)], xn[:, i % 2, bass.ts(c, P)], ident_sb[:, :])
                mm.then_inc(s_x2t_ps, 1)

            def route(i):
                pe.wait_ge(s_x2t, i + 1)
                if i >= 2:
                    pe.wait_ge(s_log, i - 1)
                for c in range(DC):
                    mm = pe.matmul(ps[:, 4 + i % 2, 0:E + 1], x2_t[:, c, bass.ts(i, P)], router_sb[:, c, :],
                                   start=(c == 0), stop=(c == DC - 1))
                mm.then_inc(s_log_ps, 1)

            for i in range(TILES + 5):
                if i < TILES:
                    project(i)
                if i >= 5:
                    route(i - 5)
                if 4 <= i < TILES + 4:
                    turn_x2(i - 4)

            def shared_up(i):
                if i >= 2:
                    pe.wait_ge(s_up, i - 1)
                if i == 0:
                    pe.wait_ge(s_ws, 16)
                    pe.wait_ge(s_x2t, TILES)
                for c in range(DC):
                    mm = pe.matmul(ps[:, 2 + i % 2, 0:GATEUP], x2_t[:, c, bass.ts(i, P)],
                                   w_ring[:, NW - 1, c * GATEUP:(c + 1) * GATEUP], start=(c == 0), stop=(c == DC - 1))
                mm.then_inc(s_sgu, 1)

            def shared_turn(i):
                pe.wait_ge(s_shid, i + 1)
                if i >= 1:
                    pe.wait_ge(s_shte, i)
                if i == 0:
                    pe.wait_ge(s_log, TILES)
                pe.transpose(ps[:, 4, 0:P], hidden[:, i % 2, :], ident_sb[:, :]).then_inc(s_sht, 1)

            def shared_down(i):
                pe.wait_ge(s_shte, i + 1)
                if i >= 1:
                    pe.wait_ge(s_sy, i)
                pe.matmul(ps[:, 5, :], hidden_t[:, i % 2, :], w_ring[:, NW - 1, DC * GATEUP:WCOLS],
                          start=True, stop=True).then_inc(s_sdn, 1)

            tables = ps[:, 7, :]

            def count_rows():
                pe.wait_ge(s_in[I_ONES], 16)
                pe.wait_ge(s_route, 1)
                pe.matmul(tables[0:E, 0:1], earlier[:, TILES, :], ones_sb[:, 0:1], start=True, stop=True).then_inc(s_cnt_ps, 1)

            def place_rows():
                for i in (I_BEFORE, I_UPTO, I_BELOW):
                    pe.wait_ge(s_in[i], 16)
                pe.wait_ge(s_cnt, 1)
                pe.matmul(tables[0:E, 8:9], upto_sb[:, :], n_col[:, 1:2], start=True, stop=True)
                pe.matmul(tables[0:1, 16:16 + E], n_col[:, 1:2], upto_sb[:, :], start=True, stop=True).then_inc(s_ends_ps, 1)
                for half in range(2):
                    o = ps[:, half, :]
                    mine = chosen[:, 8 * half:8 * half + 8, :].rearrange("p t e -> p (t e)")
                    ahead = earlier[:, 8 * half:8 * half + 8, :].rearrange("p t e -> p (t e)")
                    pe.matmul(o, before_sb[:, :], mine, start=True, stop=False)
                    pe.matmul(o, ones_sb[:, :], ahead, start=False, stop=False)
                    for k in range(8):
                        mm = pe.matmul(o[:, k * E:(k + 1) * E], n_rep, below_sb[:, :], start=False, stop=(k == 7))
                mm.then_inc(s_slots_ps, 1)

            def tile_rows():
                pe.wait_ge(s_cnt, 2)
                pe.matmul(tables[0:1, 96:96 + HIGH], ones_sb[0:E, 0:1], past_end, start=True, stop=True).then_inc(s_row_ps, 1)

            def fill_table(n):
                for m in range(n * K, (n + 1) * K):
                    pe.wait_ge(s_high, m + 1)
                    mm = pe.matmul(ps[:, 6, 0:HIGH], low_1[:, m % RING, :], high_1[:, m % RING, :],
                                   start=(m == 0), stop=(m == TILES * K - 1))
                    mm.then_inc(s_one_used, 1)

            for i in range(TILES + 1):
                if i < TILES:
                    shared_up(i)
                if i == 4:
                    place_rows()
                if i >= 1:
                    shared_turn(i - 1)
                if i == 4:
                    tile_rows()
                if i >= 1:
                    shared_down(i - 1)
                if i == 3:
                    count_rows()
                if i >= 6 and i < TILES:
                    fill_table(i - 6)
            for n in range(TILES - 6, TILES):
                fill_table(n)

            def turn_rows(t, p, r):
                pe.wait_ge(s_gather[p], r)
                if not isinstance(t, int) or t >= 2:
                    pe.wait_ge(s_xg, t - 1)
                for c in range(DC):
                    mm = pe.transpose(ps[:, p, bass.ts(c, P)], rows[:, p, bass.ts(c, P)], ident_sb[:, :])
                mm.then_inc(s_xg_ps, 1)

            slots_at = [pe.alloc_register(f"weights_slot{k}") for k in range(4)]

            def load_slots(j):
                pe.load(slots_at, ring_i[0:1, bass.ts(j, 1), :].rearrange("o j k -> o (j k)"))

            def slot_of(k):
                return pe.snap(slots_at[k], min_val=0, max_val=NW - 1)

            def up(t, p, slot):
                pe.wait_ge(s_xg, t + 1)
                for c in range(DC):
                    mm = pe.matmul(ps[:, 2 + p, 0:GATEUP], rows_t[:, p, c, :], w_ring[:, slot, c * GATEUP:(c + 1) * GATEUP],
                                   start=(c == 0), stop=(c == DC - 1))
                mm.then_inc(s_gu, 1)

            def turn_hidden(t, p):
                pe.wait_ge(s_hid, t + 1)
                pe.transpose(ps[:, 4, 0:P], hidden[:, p, :], ident_sb[:, :]).then_inc(s_ht_ps, 1)

            def down(t, p, slot):
                pe.wait_ge(s_ht, t + 1)
                pe.matmul(ps[:, 5 + p, :], hidden_t[:, p, :], w_ring[:, slot, DC * GATEUP:WCOLS],
                          start=True, stop=True).then_inc(s_dn, 1)

            pe.wait_ge(s_table, 1)
            pe.sem_inc(s_dn, 1)
            pairs = pe.value_load(pairs_i[0:1, 1:2], min_val=HIGH // 2 - TILES * 2, max_val=HIGH // 2 - 1)
            turn_rows(0, 0, 16)
            load_slots(0)
            up(0, 0, slot_of(0))
            turn_rows(1, 1, 16)
            turn_hidden(0, 0)
            up(1, 1, slot_of(1))
            with pe.Fori(0, pairs) as j:
                turn_rows(j * 2 + 2, 0, (j + 2) * 16)
                down(j * 2, 0, slot_of(0))
                turn_hidden(j * 2 + 1, 1)
                up(j * 2 + 2, 0, slot_of(2))
                turn_rows(j * 2 + 3, 1, (j + 2) * 16)
                down(j * 2 + 1, 1, slot_of(1))
                turn_hidden(j * 2 + 2, 0)
                up(j * 2 + 3, 1, slot_of(3))
                load_slots(j + 1)
            down(pairs * 2, 0, slot_of(0))

        @block.vector
        def _(dve):
            def moments_of_input(first, last):
                done, n, k = 2 * first * TB, (last - first) * TB, 2 * min(first, 1)
                for b in range(first, last):
                    dve.wait_ge(s_xin[b], 16)
                    for t in range(b * TB, (b + 1) * TB):
                        dve.bn_stats(stats[:, t, :], x_sb[:, t, :]).then_inc(s_moments, 1)
                dve.wait_ge(s_moments, done + n)
                for t in range(first * TB, last * TB):
                    dve.bn_aggr(moments[:, t, :], stats[:, t, :]).then_inc(s_moments, 1)
                dve.wait_ge(s_moments, done + 2 * n)
                variances = moments[:, first * TB:last * TB, 1]
                dve.tensor_scalar(variances, variances, EPS, None, ALU.add).then_inc(s_ln, 1)
                dve.wait_ge(s_std, k // 2 + 1)
                roots = rstd[:, first * TB:last * TB]
                dve.reciprocal(roots, roots).then_inc(s_ln, 1)
                dve.wait_ge(s_ln, k + 2)

            moments_of_input(0, 1)

            def norm_x(b4, t):
                m = b4 + t
                if not isinstance(b4, int) or t >= 2:
                    dve.wait_ge(s_xt_ps, m - 1)
                dve.tensor_scalar(xn[:, t % 2, :], x_sb[:, m, :], moments[:, m, 0:1], rstd[:, bass.ts(m, 1)],
                                  ALU.subtract, ALU.mult).then_inc(s_xn, 1)

            def take_qkt(i4, g, t):
                n = (i4 + g) * TB + t
                dve.wait_ge(s_qkt_ps, n + 1)
                dve.tensor_copy(k_t[:, g % 2, bass.ts(t, P)], turn_bank[:, P:2 * P])
                q = turn_bank[:, 0:P].rearrange("p (o n) -> p o n", o=1).broadcast_to([P, HG, P])
                hm = hmask_sb[:, :].rearrange("p (h o) -> p h o", o=1).broadcast_to([P, HG, P])
                dve.tensor_tensor(out=q_pad[:, g % 2, :, bass.ts(t, P)], in0=q, in1=hm, op=ALU.mult).then_inc(s_qkt, 1)

            dve.wait_ge(s_in[I_HMASK], 16)
            for t in range(TB):
                norm_x(0, t)
            for t in range(TB):
                take_qkt(0, 0, t)
            moments_of_input(1, B)
            dve.wait_ge(s_in[I_MASK], 16)

            def masked(b, u):
                dve.wait_ge(s_scored, b * UNITS + (u + 1))
                dve.sem_inc(s_seen, 1)
                n = (u % GU // HG + 1) * P
                sc = s_bank[u % 3][:, 0:n]
                dve.tensor_tensor_reduce(sc, sc, mask_sb[:, S - n:S], -SCALE, 3.0e38, ALU.add, ALU.min,
                                         neg_max[:, u % 4:u % 4 + 1]).then_inc(s_masked, 1)

            def normed(b, u):
                k, n = u % 4, (u % GU // HG + 1) * P
                dve.wait_ge(s_exp, b * UNITS + (u + 1))
                dve.reciprocal(rden[:, k:k + 1], den[:, k:k + 1]).then_inc(s_recip, 1)
                dve.wait_ge(s_recip, b * UNITS + (u + 1))
                dve.tensor_scalar(probs[:, k, 0:n], probs[:, k, 0:n], rden[:, k:k + 1], None, ALU.mult).then_inc(s_probs, 1)

            def batch(b, last):
                for u in range(3):
                    masked(b, u)
                for u in range(2):
                    normed(b, u)
                for u in range(UNITS):
                    g, s = divmod(u, GU)
                    if u + 3 < UNITS:
                        masked(b, u + 3)
                    if u + 2 < UNITS:
                        normed(b, u + 2)
                    if u in NORM_X_AT and not last:
                        norm_x((b + 1) * TB, NORM_X_AT.index(u))
                    for kind, t in misc_steps(g, s, last):
                        if kind == "qkt":
                            take_qkt(b * G, g + 1, t)

            every_batch(dve, batch)

            dve.wait_ge(s_in[I_COUNT], 16)
            dve.tensor_copy(count_h[:, :], count_sb[:, :]).then_inc(s_own, 1)

            own = [1]

            def step(ins):
                own[0] += 1
                ins.then_inc(s_own, 1)
                dve.wait_ge(s_own, own[0])

            def mark(ins):
                own[0] += 1
                ins.then_inc(s_own, 1)
                return own[0]

            for i in range(TILES + 3):
                a, b, r, c = i, i - 1, i - 2, i - 3
                if a < TILES:
                    dve.wait_ge(s_y_ps, a + 1)
                    stats_done = mark(dve.bn_stats(stats[:, a, :], ps[:, a % 2, :]))
                if 0 <= b < TILES:
                    small_b = small[:, b % 4, :]
                    dve.wait_ge(s_sq, attention_roots(b))
                    inverse_b = mark(dve.reciprocal(small_b[:, 3:4], small_b[:, 2:3]))
                if a < TILES:
                    small_a = small[:, a % 4, :]
                    dve.wait_ge(s_own, stats_done)
                    moments_done = mark(dve.bn_aggr(small_a[:, 0:2], stats[:, a, :]))
                if 0 <= b < TILES:
                    dve.wait_ge(s_own, inverse_b)
                    dve.tensor_scalar(delta[:, b % 2, :], ps[:, b % 2, :], small_b[:, 0:1], small_b[:, 3:4],
                                      ALU.subtract, ALU.mult).then_inc(s_stat, 1)
                if a < TILES:
                    dve.wait_ge(s_own, moments_done)
                    dve.tensor_scalar(small_a[:, 1:2], small_a[:, 1:2], EPS, None, ALU.add).then_inc(s_var, 1)
                if 0 <= c < TILES:
                    small_c = small[:, c % 4, :]
                    dve.wait_ge(s_sq, residual_roots(c))
                    inverse_c = mark(dve.reciprocal(small_c[:, 7:8], small_c[:, 6:7]))
                if 0 <= r < TILES:
                    dve.wait_ge(s_x1, r + 1)
                    stats_done = mark(dve.bn_stats(stats[:, r, :], x_sb[:, r, :]))
                if 0 <= c < TILES:
                    dve.wait_ge(s_own, inverse_c)
                    if c >= 2:
                        dve.wait_ge(s_x2d[c % 2], 16 * (c // 2))
                        dve.wait_ge(s_x2t_ps, c - 1)
                    dve.tensor_scalar(xn[:, c % 2, :], x_sb[:, c, :], small_c[:, 4:5], small_c[:, 7:8],
                                      ALU.subtract, ALU.mult).then_inc(s_x2, 1)
                if 0 <= r < TILES:
                    small_r = small[:, r % 4, :]
                    dve.wait_ge(s_own, stats_done)
                    step(dve.bn_aggr(small_r[:, 4:6], stats[:, r, :]))
                    dve.tensor_scalar(small_r[:, 5:6], small_r[:, 5:6], EPS, None, ALU.add).then_inc(s_var, 1)
            dve.wait_ge(s_log, TILES)

            step(dve.tensor_reduce(rt[:, 0, :], logits[:, :, 0:E], AX.X, ALU.max))
            dve.tensor_scalar(rt[:, 0, :], rt[:, 0, :], -1.0, None, ALU.mult).then_inc(s_neg, 1)
            dve.memset(earlier[:, 0, :], 0.0).then_inc(s_own, 1)
            own[0] += 1
            dve.wait_ge(s_e1, TILES + 1)
            step(dve.reciprocal(rt[:, 2, :], rt[:, 1, :]))
            step(dve.tensor_scalar(rt[:, 4, :], rt[:, 4, :], 1.0, None, ALU.add))
            dve.reciprocal(rt[:, 4, :], rt[:, 4, :]).then_inc(s_sigmoid, 1)

            def per_tile(a):
                return a.rearrange("p (t o) -> p t o", o=1).broadcast_to([P, TILES, E])

            step(dve.tensor_tensor(out=prob_e, in0=prob_e, in1=per_tile(rt[:, 2, :]), op=ALU.mult))
            for i in range(TILES):
                dve.max(top[:, i, :], prob_e[:, i, :]).then_inc(s_own, 1)
            own[0] += TILES
            dve.wait_ge(s_own, own[0])
            for i in range(TILES):
                dve.match_replace(prob_r[:, i, :], top[:, i, :], prob_e[:, i, :], -1.0).then_inc(s_own, 1)
            own[0] += TILES
            dve.wait_ge(s_own, own[0])
            step(dve.tensor_scalar(chosen, prob_r, -1.0, None, ALU.is_equal))
            for i in range(TILES):
                ins = dve.tensor_tensor(out=earlier[:, i + 1, :], in0=earlier[:, i, :], in1=chosen[:, i, :], op=ALU.add)
                if i < TILES - 1:
                    step(ins)
            ins.then_inc(s_route, 1)
            step(dve.tensor_reduce(rt[:, 3, :], top[:, :, :], AX.X, ALU.add))
            step(dve.reciprocal(rt[:, 3, :], rt[:, 3, :]))
            step(dve.tensor_tensor(out=prob_e, in0=prob_e, in1=chosen, op=ALU.mult))
            dve.tensor_tensor(out=prob_e, in0=prob_e, in1=per_tile(rt[:, 3, :]), op=ALU.mult).then_inc(s_comb, 1)

            dve.wait_ge(s_cnt_ps, 1)
            dve.wait_ge(s_in[I_STEPS], 16)
            dve.wait_ge(s_in[I_ONES], 16)
            dve.wait_ge(s_in[I_TOKEN], 16)
            step(dve.tensor_copy(n_col[:, 0:1], ps[0:E, 7, 0:1]))
            step(dve.tensor_scalar(n_cmp[:, :], steps_sb[:, :], n_col[:, 0:1], None, ALU.is_lt))
            step(dve.tensor_reduce(n_col[:, 1:2], n_cmp[:, :], AX.X, ALU.add))
            step(dve.tensor_scalar(n_col[:, 1:2], n_col[:, 1:2], 1.0, None, ALU.max))
            dve.tensor_scalar(n_rep, ones_sb[0:E, :], n_col[:, 1:2], None, ALU.mult).then_inc(s_cnt, 1)
            dve.wait_ge(s_ends_ps, 1)
            dve.tensor_copy(n_col[:, 2:3], ps[0:E, 7, 8:9]).then_inc(s_own, 1)
            dve.tensor_scalar(ends_i[:, :], ps[0:1, 7, 16:16 + E], 1.0, None, ALU.add).then_inc(s_tables, 1)
            own[0] += 1
            step(dve.tensor_copy(pairs_i[:, 0:1], ps[0:1, 7, 15 + E:16 + E]))
            dve.tensor_scalar(past_end, count_sb[0:E, :], n_col[:, 2:3], None, ALU.is_ge).then_inc(s_cnt, 1)
            dve.tensor_scalar(pairs_i[:, 1:2], pairs_i[:, 0:1], 1, None, ALU.logical_shift_right).then_inc(s_tables, 1)
            dve.wait_ge(s_slots_ps, 1)
            for half in range(2):
                dve.scalar_tensor_tensor(out=slots[:, 8 * half:8 * half + 8, :],
                                         in0=ps[:, half, :].rearrange("p (t e) -> p t e", e=E), scalar=1.0,
                                         in1=chosen[:, 8 * half:8 * half + 8, :], op0=ALU.add,
                                         op1=ALU.mult).then_inc(s_own, 1)
            own[0] += 2
            dve.wait_ge(s_own, own[0])
            for i in range(TILES):
                dve.max(slot_f[:, i, :], slots[:, i, :]).then_inc(s_own, 1)
            own[0] += TILES
            dve.wait_ge(s_own, own[0])
            step(dve.tensor_scalar(slot_i[:, :, :], slot_f[:, :, :], -1.0, None, ALU.add))
            dve.tensor_scalar(part_i[:, 0], slot_i[:, :, :], P - 1, None, ALU.bitwise_and).then_inc(s_own, 1)
            dve.tensor_scalar(part_i[:, 1], slot_i[:, :, :], 7, None, ALU.logical_shift_right).then_inc(s_own, 1)
            own[0] += 2
            dve.wait_ge(s_own, own[0])
            step(dve.tensor_copy(part_f[:, :, :, :], part_i[:, :, :, :]))
            dve.wait_ge(s_row_ps, 1)
            tile_expert = ps[0:1, 7, 96:96 + HIGH]
            step(dve.tensor_scalar(col_i[:, :], tile_expert, float(E - 1), None, ALU.min))
            dve.tensor_scalar(weights_i[:, :], tile_expert, float(E - 1), 1.0, ALU.min, ALU.add).then_inc(s_tables, 1)
            two_by_two = col_i[:, :].rearrange("o (j k) -> o j k", k=2)
            step(dve.tensor_scalar(ring_i[:, :, 0:2], two_by_two, NW - 1, None, ALU.bitwise_and))
            dve.tensor_scalar(ring_i[:, 0:HIGH // 2 - 1, 2:4], two_by_two[:, 1:, :], NW - 1, None,
                              ALU.bitwise_and).then_inc(s_own, 1)
            own[0] += 1
            dve.memset(ring_i[:, HIGH // 2 - 1, 2:4], 0).then_inc(s_tables, 1)
            for m in range(TILES * K):
                t, k = divmod(m, K)
                if m >= RING:
                    dve.wait_ge(s_one_used, m - RING + 1)
                dve.tensor_scalar(low_1[:, m % RING, :], count_h[:, 0:P], part_f[:, 0, t, k:k + 1], None, ALU.is_equal)
                dve.tensor_scalar(high_1[:, m % RING, :], count_h[:, :], part_f[:, 1, t, k:k + 1], token_sb[:, t:t + 1],
                                  ALU.is_equal, ALU.mult).then_inc(s_high, 1)
            dve.wait_ge(s_one_used, TILES * K)
            step(dve.tensor_copy(table_f, ps[:, 6, 0:HIGH]))
            step(dve.tensor_scalar(table_z, table_f, 0.0, float(B * S + 1), ALU.is_equal, ALU.mult))
            step(dve.scalar_tensor_tensor(out=token_i[:, 0:HIGH], in0=table_f, scalar=-1.0, in1=table_z,
                                          op0=ALU.add, op1=ALU.add))
            dve.memset(token_i[:, HIGH:HIGH + 2], B * S).then_inc(s_table, 1)

            dve.wait_ge(s_table, 1)
            dve.wait_ge(s_tables, 4)
            wcol = small[:, 0, 0:2]
            pairs = dve.value_load(pairs_i[0:1, 1:2], min_val=HIGH // 2 - TILES * 2, max_val=HIGH // 2 - 1)

            def stage_gather(t, p):
                dve.tensor_scalar(idx[:, p, 0:1], token_i[:, bass.ts(t, 1)], B * S - 1, None, ALU.min).then_inc(s_idx, 1)

            def expert_of(t):
                return dve.value_load(col_i[0:1, bass.ts(t, 1)], min_val=0, max_val=E - 1)

            def weight(t, p, r, col):
                dve.wait_ge(s_gather[p], r)
                dve.tensor_scalar(wcol[:, p:p + 1], rows[:, p, D:XROW][:, bass.ts(col, 1)], 1.0, None,
                                  ALU.mult).then_inc(s_weight, 1)

            def hide(t, p):
                dve.wait_ge(s_gate, t + 1)
                dve.wait_ge(s_weight, t + 1)
                dve.scalar_tensor_tensor(out=hidden[:, p, :], in0=gate[:, p, :], scalar=wcol[:, p:p + 1],
                                         in1=ps[:, 2 + p, F:GATEUP], op0=ALU.mult, op1=ALU.mult).then_inc(s_hid, 1)

            def take_y(t, p, r):
                dve.wait_ge(s_dn, t + 2)
                dve.wait_ge(s_scatter[p], r)
                dve.tensor_scalar(idx[:, p, 1:2], token_i[:, bass.ts(t, 1)], 0, None, ALU.add)
                dve.tensor_scalar(y_sb[:, p, :], ps[:, 5 + p, :], 1.0, None, ALU.mult).then_inc(s_y, 1)

            def take_hidden(t, p):
                dve.wait_ge(s_ht_ps, t + 1)
                dve.tensor_scalar(hidden_t[:, p, :], ps[:, 4, 0:P], 1.0, None, ALU.mult).then_inc(s_ht, 1)

            stage_gather(0, 0)
            stage_gather(1, 1)
            weight(0, 0, 16, expert_of(0))
            stage_gather(2, 0)
            hide(0, 0)
            weight(1, 1, 16, expert_of(1))
            stage_gather(3, 1)
            take_hidden(0, 0)
            with dve.Fori(0, pairs) as j:
                for p in range(2):
                    t = j * 2 + (p + 1)
                    col = expert_of(t + 1)
                    hide(t, 1 - p)
                    dve.wait_ge(s_hid, t)
                    weight(t + 1, p, (j + 2) * 16, col)
                    take_y(t - 1, p, (j + 2) * 16)
                    stage_gather(t + 3, p)
                    take_hidden(t, 1 - p)
            take_y(pairs * 2, 0, (pairs + 2) * 16)

            def gather_sum(i):
                y = y_shared[:, i, :]
                b, t = divmod(i, TB)
                step(dve.tensor_tensor(out=y, in0=y, in1=sums[:, b % 2, 0, t, :], op=ALU.add))
                dve.tensor_tensor(out=y, in0=y, in1=sums[:, b % 2, 1, t, :], op=ALU.add).then_inc(s_sum, 1)

            def last_scales(b):
                dve.wait_ge(s_lnf, b + 1)
                roots, means = rstd[:, bass.ts(b, TB)], moments[:, bass.ts(b, TB), 0]
                step(dve.reciprocal(roots, roots))
                dve.scalar_tensor_tensor(out=means, in0=means, scalar=-1.0, in1=roots, op0=ALU.mult,
                                         op1=ALU.mult).then_inc(s_lnd, 1)

            dve.wait_ge(s_sy, TILES)
            for b in range(B):
                dve.wait_ge(s_sums[b], 32)
                for t in range(TB):
                    gather_sum(b * TB + t)
                    if t == 0 and b >= 1:
                        last_scales(b - 1)
                dve.wait_ge(s_sum, (b + 1) * TB)
                for i in range(b * TB, (b + 1) * TB):
                    dve.bn_stats(stats[:, i, :], y_shared[:, i, :]).then_inc(s_own, 1)
                own[0] += TB
                dve.wait_ge(s_own, own[0])
                for i in range(b * TB, (b + 1) * TB):
                    dve.bn_aggr(moments[:, i, :], stats[:, i, :]).then_inc(s_own, 1)
                own[0] += TB
                dve.wait_ge(s_own, own[0])
                variances = moments[:, bass.ts(b, TB), 1]
                dve.tensor_scalar(variances, variances, EPS, None, ALU.add).then_inc(s_lnb, 1)
            last_scales(B - 1)
            for i in LAST_ON_DVE:
                dve.wait_ge(s_norm, i + 1)
                dve.tensor_tensor(out=x_sb[:, i, :], in0=x_sb[:, i, :], in1=y_shared[:, i, :],
                                  op=ALU.add).then_inc(s_fin_dve, 1)


def _constants():
    idx = np.arange(0, DH, 2, dtype=np.float32)
    inv_freq = (np.float32(THETA) ** (-idx / np.float32(DH))).astype(np.float32)
    angles = np.arange(S, dtype=np.float32)[:, None] * inv_freq[None, :]
    cos, sin = np.cos(angles).astype(np.float32), np.sin(angles).astype(np.float32)
    rope = np.concatenate([np.repeat(cos, 2, axis=1), -sin, sin], axis=1)
    rope = np.ascontiguousarray(rope.reshape(TB, P, 2 * DH).transpose(1, 0, 2))
    mask = np.zeros((P, S), np.float32)
    mask[:, S - P:] = np.where(np.arange(P)[None, :] > np.arange(P)[:, None], MASKED, 0.0)
    headmask = (np.arange(P)[:, None] // DH == np.arange(HG)[None, :]).astype(np.float32)
    p = np.arange(P)
    e = np.arange(E)
    tables = {
        "rope": rope, "mask": mask, "headmask": headmask, "ident": np.eye(P),
        "before": p[:, None] < p[None, :],
        "ones": np.ones((P, P)),
        "upto": e[:, None] <= e[None, :],
        "below": P * (e[:, None] < e[None, :]),
        "steps": np.broadcast_to(P * np.arange(TILES), (E, TILES)),
        "count": np.broadcast_to(np.arange(HIGH), (P, HIGH)),
        "token": p[:, None] + P * np.arange(TILES)[None, :] + 1,
    }
    return {n: np.ascontiguousarray(t, dtype=np.float32) for n, t in tables.items()}


def kernel(L0_attn_x, L0_attn_Wq, L0_attn_Wk, L0_attn_Wv, L0_attn_Wo, L0_ffn_router_w, L0_ffn_Wg, L0_ffn_Wu,
           L0_ffn_Wd, L0_ffn_Wsg, L0_ffn_Wsu, L0_ffn_Wsd, L0_ffn_Wse):
    import concourse.bacc as bacc
    from concourse.bass_utils import run_bass_kernel_spmd

    def chunks(w):
        w = np.asarray(w)
        return w.T.reshape(-1, P, w.shape[0]).transpose(1, 0, 2)

    qkv = np.stack([chunks(w).reshape(P, DC, G, P) for w in (L0_attn_Wq, L0_attn_Wk, L0_attn_Wv)], axis=3)
    wg = np.concatenate([np.asarray(L0_ffn_Wg), np.asarray(L0_ffn_Wsg)[None]])
    wu = np.concatenate([np.asarray(L0_ffn_Wu), np.asarray(L0_ffn_Wsu)[None]])
    wd = np.concatenate([np.asarray(L0_ffn_Wd), np.asarray(L0_ffn_Wsd)[None]])
    up = np.concatenate([wg, wu], axis=1).transpose(0, 2, 1).reshape(E + 1, DC, P, GATEUP).transpose(0, 2, 1, 3)
    experts = np.concatenate([up.reshape(E + 1, P, DC * GATEUP), wd.transpose(0, 2, 1)], axis=2)
    arrays = {
        "x": np.asarray(L0_attn_x).reshape(B * S, D),
        "wqkv": qkv.reshape(P, DC, G, QKV),
        "wo": chunks(L0_attn_Wo),
        "router": chunks(np.concatenate([np.asarray(L0_ffn_router_w), np.asarray(L0_ffn_Wse)])),
        "experts": experts,
        **_constants(),
    }
    arrays = {n: np.ascontiguousarray(a) for n, a in arrays.items()}
    nc = bacc.Bacc("TRN2", target_bir_lowering=False, num_devices=1)
    args = [nc.dram_tensor(n, a.shape, mybir.dt.from_np(a.dtype), kind="ExternalInput").ap() for n, a in arrays.items()]
    out = nc.dram_tensor("out", (B * S, D), FP32, kind="ExternalOutput").ap()
    sandwich_kernel(nc, *args, out)
    r = run_bass_kernel_spmd(nc, [arrays], core_ids=[0])
    return r.results[0]["out"].reshape(B, S, D)
```
